# Optimizing a Trainium2 kernel written in Bass

```python
import numpy as np
import jax
import jax.numpy as jnp

def _softmax(x, axis=-1):
    return jax.nn.softmax(x, axis=axis)

def _gelu(x):
    return jax.nn.gelu(x, approximate=True)

def _silu(x):
    return jax.nn.silu(x)

def _sigmoid(x):
    return jax.nn.sigmoid(x)

def _layernorm(x, axis=-1, eps=1e-05):
    m = jnp.mean(x, axis=axis, keepdims=True)
    v = jnp.var(x, axis=axis, keepdims=True)
    return (x - m) / jnp.sqrt(v + eps)

def _scatter_add(tgt, idx, src, axis=0):
    return tgt.at[idx].add(src)

def _segment_sum(src, seg, n):
    return jax.ops.segment_sum(src, seg, n)
kernel_name = 'mk_flamingo_gated_d1_seqx_r4_7f3bf9'

def setup_inputs(seed: int=0):
    np.random.seed(seed)
    _w = jnp.asarray

    def _rec_inputs():
        import jax
        import jax.numpy as jnp
        _rk = jax.random.key(seed)
        x = -0.0003929 + 0.9999 * jax.random.normal(jax.random.fold_in(_rk, 1), (8, 512, 512), jnp.float32)
        _lenS = 512 - jax.random.randint(jax.random.fold_in(_rk, 7), (8,), 0, max(1, 512 // 4) + 1, jnp.int32)
        _lenS2 = 64 - jax.random.randint(jax.random.fold_in(_rk, 8), (8,), 0, max(1, 64 // 4) + 1, jnp.int32)
        _ctx_1024P = jax.random.normal(jax.random.fold_in(_rk, 11), (8, 16, 256), jnp.float32)
        _ctx_1024c = jax.random.dirichlet(jax.random.fold_in(_rk, 511), 0.3 * jnp.ones((16,), jnp.float32), (8, 64))
        _ctx_1024t = jnp.einsum('bsk,bkd->bsd', _ctx_1024c, _ctx_1024P)
        _ctx_1024t = _ctx_1024t * jax.lax.rsqrt(jnp.mean(jnp.square(_ctx_1024t)) + 1e-12) * 0.953939
        ctx_1024 = -0.000494167 + 1.00018 * (_ctx_1024t + 0.3 * jax.random.normal(jax.random.fold_in(_rk, 611), (8, 64, 256), jnp.float32))
        _validS = jnp.arange(512)[None, :] < _lenS[:, None]
        _validS2 = jnp.arange(64)[None, :] < _lenS2[:, None]
        _causal = jnp.tril(jnp.ones((512, 512), dtype=bool))
        mask_BxS2_bf1 = jnp.ones((8, 64), dtype=bool)
        _g = jax.random.normal(jax.random.fold_in(_rk, 9001), (2, 1), jnp.float32)
        _g = jnp.sign(_g) * jnp.maximum(jnp.abs(_g), 1.0) + (_g == 0) * 1.0
        g_xattn = _g[0]
        g_ffn = _g[1]
        return (x, ctx_1024, mask_BxS2_bf1, g_xattn, g_ffn)
    x, ctx_1024, mask_BxS2_bf1, g_xattn, g_ffn = _rec_inputs()

    def _L0_xattn_setup():
        import jax, jax.numpy as jnp
        import numpy as np
        N_HEADS = 16
        N_KV_HEADS = 8
        HEAD_DIM = 128
        D_TEXT = 512
        D_VISION = 256
        GROUPS = N_HEADS // N_KV_HEADS
        key = jax.random.key(seed)
        ks = jax.random.split(key, 6)
        B, T_text, T_vis = (4, 512, 144)
        text_hidden = jax.random.normal(ks[0], (B, T_text, D_TEXT), dtype=jnp.float32)
        vision_tokens = jax.random.normal(ks[1], (B, T_vis, D_VISION), dtype=jnp.float32)
        vision_mask = jnp.ones((B, T_vis), dtype=bool)
        s = 0.02
        Wq = jax.random.normal(ks[2], (D_TEXT, N_HEADS * HEAD_DIM), dtype=jnp.float32) * s
        Wk = jax.random.normal(ks[3], (D_VISION, N_KV_HEADS * HEAD_DIM), dtype=jnp.float32) * s
        Wv = jax.random.normal(ks[4], (D_VISION, N_KV_HEADS * HEAD_DIM), dtype=jnp.float32) * s
        Wo = jax.random.normal(ks[5], (N_HEADS * HEAD_DIM, D_TEXT), dtype=jnp.float32) * s
        return {'text_hidden': text_hidden, 'vision_tokens': vision_tokens, 'vision_mask': vision_mask, 'Wq': Wq, 'Wk': Wk, 'Wv': Wv, 'Wo': Wo}
    _L0_xattn_all = _L0_xattn_setup()
    _L0_xattn_in = {k: v for k, v in _L0_xattn_all.items() if k in ('Wq', 'Wk', 'Wv', 'Wo')}
    del _L0_xattn_all

    def _L0_ffn_setup():
        import jax, jax.numpy as jnp
        import numpy as np
        H = 512
        I = 256
        E = 32
        K = 4
        N_SHARED = 1
        EPS = 1e-06

        def _rmsnorm(x, w, eps=EPS):
            var = jnp.mean(jnp.square(x), axis=-1, keepdims=True)
            return x * jax.lax.rsqrt(var + eps) * w

        def _moe_core(x, gate_w, w13, w2):
            T = x.shape[0]
            N = T * K
            C = 2 * N // E
            logits = jnp.einsum('th,eh->te', x.astype(jnp.float32), gate_w.astype(jnp.float32))
            scores = jax.nn.softmax(logits, axis=-1)
            topk_w, topk_ids = jax.lax.top_k(scores, K)
            topk_w = topk_w / jnp.sum(topk_w, axis=-1, keepdims=True)
            flat_ids = topk_ids.reshape(-1)
            flat_w = topk_w.reshape(-1)
            order = jnp.argsort(flat_ids)
            sorted_eid = flat_ids[order]
            tok = order // K
            counts = jnp.zeros((E,), jnp.int32).at[flat_ids].add(1)
            starts = jnp.cumsum(counts) - counts
            pos = jnp.arange(N) - starts[sorted_eid]
            buf = jnp.zeros((E, C, x.shape[1]), x.dtype).at[sorted_eid, pos].set(x[tok], mode='drop')
            gu = jnp.einsum('ech,ehf->ecf', buf, w13)
            g, u = jnp.split(gu, 2, axis=-1)
            act = jax.nn.silu(g) * u
            eo = jnp.einsum('eci,eih->ech', act, w2)
            out_slots = eo[sorted_eid, pos]
            routed = jnp.zeros_like(x).at[tok].add(out_slots * flat_w[order][:, None])
            return routed
        key = jax.random.key(seed)
        ks = jax.random.split(key, 8)
        s = 1.0 / np.sqrt(H)
        si = 1.0 / np.sqrt(I)
        return {'hidden_states': jax.random.normal(ks[0], (1, 1024, H), jnp.float32), 'norm_w': jnp.ones((H,), jnp.float32), 'gate_w': jax.random.normal(ks[1], (E, H), jnp.float32) * s, 'w13': jax.random.normal(ks[2], (E, H, 2 * I), jnp.float32) * s, 'w2': jax.random.normal(ks[3], (E, I, H), jnp.float32) * si, 'shared_gate_w': jax.random.normal(ks[4], (H, I * N_SHARED), jnp.float32) * s, 'shared_up_w': jax.random.normal(ks[5], (H, I * N_SHARED), jnp.float32) * s, 'shared_down_w': jax.random.normal(ks[6], (I * N_SHARED, H), jnp.float32) * si}
    _L0_ffn_all = _L0_ffn_setup()
    _L0_ffn_in = {k: v for k, v in _L0_ffn_all.items() if k in ('norm_w', 'gate_w', 'w13', 'w2', 'shared_gate_w', 'shared_up_w', 'shared_down_w')}
    del _L0_ffn_all
    return {'x': x, 'ctx_1024': ctx_1024, 'mask_BxS2_bf1': mask_BxS2_bf1, 'g_xattn': g_xattn, 'g_ffn': g_ffn, 'L0_xattn_Wq': _L0_xattn_in['Wq'], 'L0_xattn_Wk': _L0_xattn_in['Wk'], 'L0_xattn_Wv': _L0_xattn_in['Wv'], 'L0_xattn_Wo': _L0_xattn_in['Wo'], 'L0_ffn_norm_w': _L0_ffn_in['norm_w'], 'L0_ffn_gate_w': _L0_ffn_in['gate_w'], 'L0_ffn_w13': _L0_ffn_in['w13'], 'L0_ffn_w2': _L0_ffn_in['w2'], 'L0_ffn_shared_gate_w': _L0_ffn_in['shared_gate_w'], 'L0_ffn_shared_up_w': _L0_ffn_in['shared_up_w'], 'L0_ffn_shared_down_w': _L0_ffn_in['shared_down_w']}

def reference(x, ctx_1024, mask_BxS2_bf1, g_xattn, g_ffn, L0_xattn_Wq, L0_xattn_Wk, L0_xattn_Wv, L0_xattn_Wo, L0_ffn_norm_w, L0_ffn_gate_w, L0_ffn_w13, L0_ffn_w2, L0_ffn_shared_gate_w, L0_ffn_shared_up_w, L0_ffn_shared_down_w):
    import jax
    import jax.numpy as jnp

    def _L0_xattn_ref(text_hidden, vision_tokens, vision_mask, Wq, Wk, Wv, Wo):
        import jax, jax.numpy as jnp
        import numpy as np
        N_HEADS = 16
        N_KV_HEADS = 8
        HEAD_DIM = 128
        D_TEXT = 512
        D_VISION = 256
        GROUPS = N_HEADS // N_KV_HEADS
        B, T_text, _ = text_hidden.shape
        T_vis = vision_tokens.shape[1]
        scale = jnp.float32(np.sqrt(HEAD_DIM))
        q = (text_hidden @ Wq).reshape(B, T_text, N_HEADS, HEAD_DIM).transpose(0, 2, 1, 3)
        k = (vision_tokens @ Wk).reshape(B, T_vis, N_KV_HEADS, HEAD_DIM).transpose(0, 2, 1, 3)
        v = (vision_tokens @ Wv).reshape(B, T_vis, N_KV_HEADS, HEAD_DIM).transpose(0, 2, 1, 3)
        k = jnp.repeat(k, GROUPS, axis=1)
        v = jnp.repeat(v, GROUPS, axis=1)
        scores = jnp.einsum('bhtd,bhsd->bhts', q, k) / scale
        mask = vision_mask[:, None, None, :]
        scores = jnp.where(mask, scores, -jnp.inf)
        attn = jax.nn.softmax(scores, axis=-1)
        attn = jnp.nan_to_num(attn, nan=0.0)
        out = jnp.einsum('bhts,bhsd->bhtd', attn, v)
        out = out.transpose(0, 2, 1, 3).reshape(B, T_text, N_HEADS * HEAD_DIM)
        return out @ Wo

    def _L0_ffn_ref(hidden_states, norm_w, gate_w, w13, w2, shared_gate_w, shared_up_w, shared_down_w):
        import jax, jax.numpy as jnp
        import numpy as np
        H = 512
        I = 256
        E = 32
        K = 4
        N_SHARED = 1
        EPS = 1e-06

        def _rmsnorm(x, w, eps=EPS):
            var = jnp.mean(jnp.square(x), axis=-1, keepdims=True)
            return x * jax.lax.rsqrt(var + eps) * w

        def _moe_core(x, gate_w, w13, w2):
            T = x.shape[0]
            N = T * K
            C = 2 * N // E
            logits = jnp.einsum('th,eh->te', x.astype(jnp.float32), gate_w.astype(jnp.float32))
            scores = jax.nn.softmax(logits, axis=-1)
            topk_w, topk_ids = jax.lax.top_k(scores, K)
            topk_w = topk_w / jnp.sum(topk_w, axis=-1, keepdims=True)
            flat_ids = topk_ids.reshape(-1)
            flat_w = topk_w.reshape(-1)
            order = jnp.argsort(flat_ids)
            sorted_eid = flat_ids[order]
            tok = order // K
            counts = jnp.zeros((E,), jnp.int32).at[flat_ids].add(1)
            starts = jnp.cumsum(counts) - counts
            pos = jnp.arange(N) - starts[sorted_eid]
            buf = jnp.zeros((E, C, x.shape[1]), x.dtype).at[sorted_eid, pos].set(x[tok], mode='drop')
            gu = jnp.einsum('ech,ehf->ecf', buf, w13)
            g, u = jnp.split(gu, 2, axis=-1)
            act = jax.nn.silu(g) * u
            eo = jnp.einsum('eci,eih->ech', act, w2)
            out_slots = eo[sorted_eid, pos]
            routed = jnp.zeros_like(x).at[tok].add(out_slots * flat_w[order][:, None])
            return routed
        B, S, Hd = hidden_states.shape
        residual = hidden_states
        h = _rmsnorm(hidden_states, norm_w)
        x = h.reshape(-1, Hd)
        routed = _moe_core(x, gate_w, w13, w2)
        shared = jax.nn.silu(x @ shared_gate_w) * (x @ shared_up_w) @ shared_down_w
        out = residual + (routed + shared).reshape(B, S, Hd)
        return out
    x = x + jnp.tanh(g_xattn[0]) * _L0_xattn_ref(_layernorm(x, axis=-1), ctx_1024, mask_BxS2_bf1, L0_xattn_Wq, L0_xattn_Wk, L0_xattn_Wv, L0_xattn_Wo)
    x = x + jnp.tanh(g_ffn[0]) * _L0_ffn_ref(_layernorm(x, axis=-1), L0_ffn_norm_w, L0_ffn_gate_w, L0_ffn_w13, L0_ffn_w2, L0_ffn_shared_gate_w, L0_ffn_shared_up_w, L0_ffn_shared_down_w)
    return x

_drawn_inputs = setup_inputs


def setup_inputs(seed=0):
    import zlib

    import numpy as np

    out = dict(_drawn_inputs(seed))
    spreads = {'L0_ffn_norm_w': (1.0, 0.2)}
    factors = {}
    for name, (base, spread) in spreads.items():
        noise = np.random.default_rng([zlib.crc32(name.encode()), seed]).standard_normal(out[name].shape)
        drawn = base * np.exp(spread * noise) if base else spread * noise
        out[name] = jnp.asarray(drawn.astype(out[name].dtype))
    for name, factor in factors.items():
        out[name] = (out[name] * factor).astype(out[name].dtype)
    return out
```

```python
import concourse.bass as bass
from concourse import mybir
from contextlib import ExitStack

F32 = mybir.dt.float32
F32R = mybir.dt.float32r
BF16 = mybir.dt.bfloat16
I32 = mybir.dt.int32
U32 = mybir.dt.uint32
U8 = mybir.dt.uint8
ALU = mybir.AluOpType
ACT = mybir.ActivationFunctionType
AX_X = mybir.AxisListType.X

P = 128
B, T, D = 8, 512, 512
S, DV = 64, 256
H, G, DH = 16, 8, 128
E, K, I = 32, 4, 256
N = B * T
TILES = N // P
TPB = T // P
DC = D // P
IC = I // P
HS = H * S
HC = HS // P
CAP = 2 * N * K // E
BLK = N // P
PADBLK = E * BLK
MT = N * K // P + E
MTP = 2 * P
SCALE = float(DH) ** -0.5
LN_EPS, RMS_EPS = 1e-5, 1e-6
SQUASH = 1e30
ARENA = 128 * 1024


def ap(t, offset, dims):
    return bass.AP(tensor=t[:].tensor, offset=offset, ap=dims)


class Count:

    def __init__(self, eng, sem):
        self.eng, self.sem, self.n = eng, sem, 0

    def done(self, ins):
        self.n += 1
        ins.then_inc(self.sem, 1)
        self.eng.wait_ge(self.sem, self.n)

    def restart(self):
        if self.n:
            self.eng.wait_ge(self.sem, self.n)
            self.eng.sem_inc(self.sem, -self.n)
            self.n = 0


def wait(eng, sem, value):
    if not isinstance(value, int) or value > 0:
        eng.wait_ge(sem, value)


def token_steps(eng, body, counts=()):
    for j in range(TPB):
        body(0, j)
    for c in counts:
        c.restart()
    with eng.Fori(1, B) as beta:
        for j in range(TPB):
            body(beta, j)
        for c in counts:
            c.restart()
    for j in range(TPB):
        body(B, j)


def tile_at(beta, j, lag):
    t = TPB * beta + (j - lag)
    if isinstance(t, int) and not 0 <= t < TILES:
        return None
    return t


def batch_of(beta, j, lag):
    return beta + (j - lag) // TPB


def flamingo(nc, x, ctx, mask, g_xattn, g_ffn, wq, wk, wv, wo, norm_w, gate_w, w13, w2, sg, su, sdn, out):
    es = ExitStack()
    nc.disable_value_cache = True
    with es:
        base = (nc.sbuf_base + 31) // 32 * 32
        es.enter_context(nc.sbuf_tensor("arena", [P, ARENA // 4], F32))
        KB = 1024

        def at(name, shape, dt, kb):
            return nc.alloc_sbuf_tensor_at(name, shape, dt, offset=base + int(kb * KB))

        def sb(name, shape, dt=F32):
            return es.enter_context(nc.sbuf_tensor(name, shape, dt))

        def dram(name, shape, dt=F32):
            return nc.dram_tensor(name, shape, dt, kind="Internal").ap()

        def sem(name):
            return es.enter_context(nc.semaphore(name))

        m_dram = dram("m_dram", (B, P, 2, DC, HS))
        vw_dram = dram("vw_dram", (B, P, 2, G, D))
        h_dram = dram("h_dram", (N, D))
        slot_dram = dram("slot_dram", ((PADBLK + 1) * P, 2))

        m_sb = at("m_sb", [P, 2, 2, DC, HS], F32R, 0)
        vw_sb = at("vw_sb", [P, 2, 2, G, D], F32R, 64)
        vw_st = at("vw_st", [P, 2, 2, 2, B // 2, D], F32R, 0)
        m_st = at("m_st", [P, 2, B * HS], F32R, 0)
        kt = at("kt", [P, G, B * S], F32, 64)
        wqc = at("wqc", [P, 2, H * DH], F32, 80)
        wqt = at("wqt", [P, H * P], F32, 96)
        ctx_sb = at("ctx_sb", [P, 4, DV], F32, 104)
        ctxt = at("ctxt", [P, 2, B * S], F32, 108)
        wkg = at("wkg", [P, 2, 2, DH], F32, 112)
        wvg = at("wvg", [P, 2, 2, DH], F32, 114)
        wog = at("wog", [P, 2, 2, D], F32, 116)
        vt = at("vt", [P, 2, B * S], F32, 124)
        ew13 = at("ew13", [P, 2, DC, 2 * I], F32, 0)
        ew2 = at("ew2", [P, 2, IC, D], F32, 16)
        hg = at("hg", [P, 4, D], F32, 24)
        hgt = at("hgt", [P, 2, D], F32, 32)
        eth = at("eth", [P, 2, I], F32, 36)
        eact = at("eact", [P, 2, I], F32, 38)
        eactt = at("eactt", [P, 2, I], F32, 40)
        ey = at("ey", [P, 4, D], F32, 42)
        blocks = at("blocks", [P, 2, 2 * P], F32, 50)
        rec4 = at("rec4", [P, 2, 4, P], F32, 54)
        dst_i = at("dst_i", [P, MTP], I32, 58)
        src_i = at("src_i", [P, MTP], I32, 59)
        wcol = at("wcol", [P, MTP], F32, 60)
        exp_i = at("exp_i", [P, MTP], I32, 61)
        tcmp = at("tcmp", [P, 2, 2, E], F32, 62)
        tsm = at("tsm", [P, 2, 16], F32, 63)
        id1023 = at("id1023", [P, 2, 2], F32, 64)
        tix = at("tix", [P, 2, 2], I32, 64.25)
        cnt = at("cnt", [P, 4, E], F32, 65)
        cnt_i = at("cnt_i", [P, 2, E], I32, 66)
        end_i = at("end_i", [P, E], I32, 67)
        src4 = at("src4", [P, 4], I32, 68)
        dst1 = at("dst1", [P, 1], I32, 68.25)

        ident = sb("ident", [P, P])
        row0 = sb("row0", [P, P], BF16)
        tri = sb("tri", [P, P], BF16)
        ones = sb("ones", [P, P], BF16)
        iota_e = sb("iota_e", [P, E])
        iota_p = sb("iota_p", [P, 1])
        gx = sb("gx", [P, 5])
        half_power = sb("half_power", [P, 2])
        mask8 = sb("mask8", [P, B * S], U8)
        mask_ft = sb("mask_ft", [P, 2, B // 2])
        mask8c = sb("mask8c", [P, 2, B // 2], U8)
        bias = sb("bias", [P, B, S], BF16)
        normw = sb("normw", [P, D])
        swg = sb("swg", [P, 2, DC, 2 * I], F32R)
        swd = sb("swd", [P, 2, IC, D], F32R)
        gtw = sb("gtw", [P, 2, DC, E], F32R)
        x_sb = sb("x_sb", [P, 4, D])
        xn = sb("xn", [P, D])
        xnt = sb("xnt", [P, 2, D], F32R)
        prob = sb("prob", [P, HS])
        pt = sb("pt", [P, 2, HS], F32R)
        x2 = sb("x2", [P, D])
        hs = sb("hs", [P, D])
        h_sb = sb("h_sb", [P, D])
        ht = sb("ht", [P, 2, D], F32R)
        sth = sb("sth", [P, I])
        sact = sb("sact", [P, I])
        sactt = sb("sactt", [P, 2, I], F32R)
        base_sb = sb("base_sb", [P, 2, D])
        st1 = sb("st1", [P, 16])
        st2 = sb("st2", [P, 24])
        mx = sb("mx", [P, 3, H])
        logit = sb("logit", [P, 2, TPB, E])
        top8 = sb("top8", [P, TPB, 8])
        idx8 = sb("idx8", [P, TPB, 8], U32)
        idxf = sb("idxf", [P, TPB, K])
        onehot = sb("onehot", [P, TPB, K, E], BF16)
        chosen = sb("chosen", [P, TPB, E], BF16)
        carry = sb("carry", [P, TPB + 1, E])
        posn = sb("posn", [P, TPB, E])
        ranks = sb("ranks", [P, 2 * TPB * E])
        rw = sb("rw", [P, 4, TPB, K])
        rws = sb("rws", [P, 4, TPB])
        rec = sb("rec", [P, TPB, K, 2])
        row_i = sb("row_i", [P, TPB, K], I32)
        tokid = sb("tokid", [P, TPB])
        wst = at("wst", [P, DC, 2 * I], F32, 96)
        bank = [es.enter_context(nc.psum_tensor(f"bank{i}", [P, 512], F32)) for i in range(8)]
        ps_s = bank[0:2]
        ps_t = bank[2:5]
        ps_od, ps_g, ps_l = bank[5], bank[6], bank[7]

        consts_made, ident_made = sem("consts_made"), sem("ident_made")
        small_loaded, masks_made, tanh_made = sem("small_loaded"), sem("masks_made"), sem("tanh_made")
        shared_loaded, shared_split = sem("shared_loaded"), sem("shared_split")
        gate_turned, gate_split = sem("gate_turned"), sem("gate_split")
        ctx_turned, ctx_copied = sem("ctx_turned"), sem("ctx_copied")
        gw_loaded = [sem("gw_loaded0"), sem("gw_loaded1")]
        kv_made, kv_copied = sem("kv_made"), sem("kv_copied")
        vw_made, vw_hi, vw_split = sem("vw_made"), sem("vw_hi"), sem("vw_split")
        vw_stored = [sem("vw_stored0"), sem("vw_stored1")]
        wq_loaded = [sem("wq_loaded0"), sem("wq_loaded1")]
        wq_turned, wq_copied = sem("wq_turned"), sem("wq_copied")
        m_made, m_hi, m_split, m_stored = sem("m_made"), sem("m_hi"), sem("m_split"), sem("m_stored")
        dve_step, pool_step = sem("dve_step"), sem("pool_step")
        slots_cleared = sem("slots_cleared")

        x_loaded = [sem(f"x_loaded{i}") for i in range(4)]
        mw_loaded = sem("mw_loaded")
        xn_ready, xt_made, xt_hi, xt_split = sem("xn_ready"), sem("xt_made"), sem("xt_hi"), sem("xt_split")
        var1_ready, ln1_ready, var2_ready = sem("var1_ready"), sem("ln1_ready"), sem("var2_ready")
        scores_made, shifted, exp_made, rinv_made, probs_ready = (
            sem("scores_made"), sem("shifted"), sem("exp_made"), sem("rinv_made"), sem("probs_ready"))
        pt_made, pt_hi, pt_split = sem("pt_made"), sem("pt_hi"), sem("pt_split")
        attn_made, x2_ready, ln2_ready, hs_ready, hn_ready, h_ready = (
            sem("attn_made"), sem("x2_ready"), sem("ln2_ready"), sem("hs_ready"), sem("hn_ready"), sem("h_ready"))
        base1_ready, h_stored = sem("base1_ready"), sem("h_stored")
        ht_made, ht_hi, ht_split = sem("ht_made"), sem("ht_hi"), sem("ht_split")
        logits_made, logits_kept, gu_made, tanh_ready, act_ready = (
            sem("logits_made"), sem("logits_kept"), sem("gu_made"), sem("tanh_ready"), sem("act_ready"))
        at_made, at_hi, at_split = sem("at_made"), sem("at_hi"), sem("at_split")
        down_made, base_ready = sem("down_made"), sem("base_ready")
        base_stored = [sem("base_stored0"), sem("base_stored1")]
        pads_stored = sem("pads_stored")
        ranks_kept = sem("ranks_kept")
        chosen_ready, ranks_made, rw_shifted, rw_exp, rows_ready, slots_written = (
            sem("chosen_ready"), sem("ranks_made"), sem("rw_shifted"), sem("rw_exp"), sem("rows_ready"),
            sem("slots_written"))
        tix_ready, blocks_loaded, rec4_ready, rec4_turned, tables_ready = (
            sem("tix_ready"), sem("blocks_loaded"), sem("rec4_ready"), sem("rec4_turned"), sem("tables_ready"))

        ew_loaded = sem("ew_loaded")
        eg_made = sem("eg_made")
        hg_loaded = [sem(f"hg_loaded{i}") for i in range(4)]
        et_made, et_copied, egu_made, eth_made, eact_made = (
            sem("et_made"), sem("et_copied"), sem("egu_made"), sem("eth_made"), sem("eact_made"))
        eat_made, eat_copied, ed_made, ey_ready, y_added = (
            sem("eat_made"), sem("eat_copied"), sem("ed_made"), sem("ey_ready"), sem("y_added"))

        def plain_wait(eng, sem, value):
            value = value if isinstance(value, int) else eng.snap(value)
            eng.wait_ge(consts_made, 2)
            eng.wait_ge(sem, value)

        x_rows = x.rearrange("b t d -> (b t) d")
        wq_rows = wq.rearrange("(c p) n -> c p n", p=P)
        def m_place(hl, h):
            e = h % 2
            return ap(m_st, hl * B * HS + (h // 2) * 2 * S + e * S,
                      [[2 * B * HS, P], [2 * HS, B // 2], [HS + (S if e == 0 else -S), 2], [1, S]])

        def valid(n):
            return not isinstance(n, int) or 0 <= n < MT

        def expert_steps(eng, body):
            for v in range(8):
                body(v, v % 4)
            with eng.Fori(2, MT // 4) as i:
                for j in range(4):
                    body(4 * i + j, j)
            for j in range(2):
                body(MT + j, j)

        block = es.enter_context(nc.Block())

        @block.sync
        def _(sp):
            sp.dma_start(ctx_sb[:], ctx.rearrange("b s d -> (b s) d").rearrange("(q p) d -> p q d", p=P)).then_inc(
                small_loaded, 16)
            sp.dma_start(gx[:, 0:1], g_xattn.rearrange("(a n) -> a n", a=1).to_broadcast([P, 1])).then_inc(small_loaded, 16)
            sp.dma_start(gx[:, 1:2], g_ffn.rearrange("(a n) -> a n", a=1).to_broadcast([P, 1])).then_inc(small_loaded, 16)
            sp.dma_start(normw[:], norm_w.rearrange("(a n) -> a n", a=1).to_broadcast([P, D])).then_inc(small_loaded, 16)
            sp.dma_start(mask8[:], mask.rearrange("b s -> (b s)").rearrange("(a n) -> a n", a=1).to_broadcast([P, B * S])
                         ).then_inc(small_loaded, 16)
            by_s = mask.rearrange("(p q) s -> s q p", q=2)
            for odd in range(2):
                for half in range(2):
                    sp.dma_start(mask8c[half * S:half * S + S, odd, :], by_s[:, half ^ odd, :],
                                 allow_slow_non_contiguous=True).then_inc(small_loaded, 16)

            def load_group(g, q):
                for dst, src in ((wkg, wk), (wvg, wv)):
                    sp.dma_start(dst[:, q], src.rearrange("(c p) (g n) -> g p c n", p=P, n=DH)[bass.ds(g, 1)].rearrange(
                        "o p c n -> p (o c) n")).then_inc(gw_loaded[q], 16)
                sp.dma_start(wog[:, q], wo.rearrange("(g e p) n -> g p e n", e=2, p=P)[bass.ds(g, 1)].rearrange(
                    "o p e n -> p (o e) n")).then_inc(gw_loaded[q], 16)

            def store_group(g, q):
                sp.wait_ge(vw_split, (B) * g + B)
                for hl in range(2):
                    for odd in range(2):
                        for half in range(2):
                            row = vw_dram[:, :, hl].rearrange("(p q) r g n -> q r p g n", q=2)[
                                half ^ odd, half * S:half * S + S]
                            sp.dma_start(row[:, :, bass.ds(g, 1), :].rearrange("r p o n -> r (p o) n"),
                                         vw_st[half * S:half * S + S, q, hl, odd].bitcast(F32)).then_inc(vw_stored[q], 16)

            load_group(0, 0)
            load_group(1, 1)
            wst_g = sg.rearrange("(c p) n -> p c n", p=P)
            sp.dma_start(wst[:, :, 0:I], wst_g).then_inc(shared_loaded, 16)
            sp.dma_start(wst[:, :, I:2 * I], su.rearrange("(c p) n -> p c n", p=P)).then_inc(shared_loaded, 16)
            sp.dma_start(x_sb[:, 0:2, :], sdn.rearrange("(c p) n -> p c n", p=P)).then_inc(shared_loaded, 16)
            sp.dma_start(x_sb[0:E, 2, :], gate_w).then_inc(shared_loaded, 16)
            sp.wait_ge(consts_made, 1)
            slot_src = prob[:, 0:2 * P]
            sp.dma_start(slot_dram[0:PADBLK * P].rearrange("(p k s) w -> p k (s w)", p=P, s=P),
                         ap(prob, 0, [[HS, P], [0, PADBLK // P], [1, 2 * P]])).then_inc(slots_cleared, 16)
            sp.dma_start(slot_dram[PADBLK * P:].rearrange("(o s) w -> o (s w)", o=1), slot_src[0:1]).then_inc(
                slots_cleared, 16)
            sp.dma_start(out[N:N + P, :], ap(prob, 2 * P, [[HS, P], [1, D]])).then_inc(pads_stored, 16)

            with sp.Fori(0, G // 2 - 1) as i:
                for q in range(2):
                    store_group(2 * i + q, q)
                    sp.wait_ge(vw_made, B * (2 * i) + B * (q + 1))
                    load_group(2 * i + q + 2, q)
            sp.dma_start(wqc[:, 0], wq_rows[0]).then_inc(wq_loaded[0], 16)
            sp.dma_start(wqc[:, 1], wq_rows[1]).then_inc(wq_loaded[1], 16)
            for g in range(G - 2, G):
                store_group(g, g % 2)
            for c in range(DC):
                sp.wait_ge(m_split, H * c + H)
                if c + 2 < DC:
                    sp.dma_start(wqc[:, c % 2], wq_rows[c + 2]).then_inc(wq_loaded[c % 2], 16)
                for hl in range(2):
                    sp.dma_start(m_dram[:, :, hl, c].rearrange("b p n -> p b n"),
                                 m_st[:, hl].bitcast(F32).rearrange("p (b n) -> p b n", b=B)).then_inc(m_stored, 16)
            for q in range(2):
                sp.wait_ge(vw_stored[q], 16 * 8 * G // 2)
            sp.wait_ge(m_stored, 32 * DC)

            def load_mw(b):
                q = b % 2
                sp.dma_start(m_sb[:, bass.ds(q, 1)].bitcast(F32).rearrange("p o h c n -> p (o h) c n"),
                             m_dram[bass.ds(b, 1)].rearrange("o p h c n -> p (o h) c n")).then_inc(mw_loaded, 16)
                sp.dma_start(vw_sb[:, bass.ds(q, 1)].bitcast(F32).rearrange("p o h g n -> p (o h) g n"),
                             vw_dram[bass.ds(b, 1)].rearrange("o p h g n -> p (o h) g n")).then_inc(mw_loaded, 16)

            sp.wait_ge(shared_split, 2)
            sp.wait_ge(gate_turned, 1)
            sp.dma_start(x_sb[:, 0], x_rows[0:P]).then_inc(x_loaded[0], 16)
            load_mw(0)
            sp.wait_ge(mw_loaded, 32)
            load_mw(1)

            def step(beta, j):
                t = tile_at(beta, j, -1)
                if t is not None:
                    wait(sp, x2_ready, t - 3)
                    sp.dma_start(x_sb[:, (j + 1) % 4], x_rows[bass.ds(t * P, P)]).then_inc(x_loaded[(j + 1) % 4], 16)
                t = tile_at(beta, j, 3)
                if t is not None:
                    sp.wait_ge(h_ready, t + 1)
                    sp.dma_start(h_dram[bass.ds(t * P, P)], h_sb[:]).then_inc(h_stored, 16)
                t = tile_at(beta, j, 4)
                if t is not None:
                    sp.wait_ge(base_ready, t + 1)
                    sp.dma_start(out[bass.ds(t * P, P)], base_sb[:, j % 2]).then_inc(base_stored[j % 2], 16)

            for j in range(TPB):
                step(0, j)
            with sp.Fori(1, B - 1) as beta:
                for j in range(TPB):
                    step(beta, j)
                    if j == 1:
                        sp.wait_ge(attn_made, beta * TPB)
                        sp.wait_ge(mw_loaded, beta * 32 + 32)
                        load_mw(beta + 1)
            for beta in (B - 1, B):
                for j in range(TPB):
                    step(beta, j)

            sp.wait_ge(attn_made, TILES)

            def load_expert(e, q):
                sp.dma_start(ew13[:, q], w13[bass.ds(e, 1)].rearrange("o (c p) n -> p (o c) n", p=P)).then_inc(ew_loaded, 16)
                sp.dma_start(ew2[:, q], w2[bass.ds(e, 1)].rearrange("o (c p) n -> p (o c) n", p=P)).then_inc(ew_loaded, 16)

            for e in range(2):
                if e:
                    sp.wait_ge(ew_loaded, 32 * e)
                load_expert(e, e)
            sp.wait_ge(tables_ready, 2)
            with sp.Fori(1, E // 2) as i:
                for q in range(2):
                    last = sp.value_load(end_i[0:1, bass.ds(2 * i + (q - 2), 1)], min_val=1, max_val=MT + 1)
                    sp.wait_ge(ew_loaded, 64 * i + 32 * q)
                    sp.wait_ge(ed_made, last)
                    load_expert(2 * i + q, q)

        @block.gpsimd
        def _(pool):
            own = Count(pool, pool_step)
            own.done(pool.memset(ident[:], 0.0))
            own.done(pool.affine_select(out=ident[:], in_=ident[:], compare_op=ALU.not_equal, fill=1.0, base=0,
                                        pattern=[[-1, P]], channel_multiplier=1))
            pool.iota(iota_e[:], pattern=[[1, E]], base=0, channel_multiplier=0,
                      allow_small_or_imprecise_dtypes=True).then_inc(ident_made, 1)
            own.done(pool.memset(prob[:], 0.0))
            pool.iota(ap(prob, 0, [[HS, P], [2, P]]), pattern=[[1, P]], base=N, channel_multiplier=0,
                      allow_small_or_imprecise_dtypes=True).then_inc(consts_made, 1)
            own.done(pool.memset(ones[:], 1.0))
            own.done(pool.affine_select(out=row0[:], in_=ones[:], compare_op=ALU.is_equal, fill=0.0, base=0,
                                        pattern=[[0, P]], channel_multiplier=1))
            own.done(pool.affine_select(out=tri[:], in_=ones[:], compare_op=ALU.is_gt, fill=0.0, base=0,
                                        pattern=[[1, P]], channel_multiplier=-1))
            own.done(pool.iota(iota_p[:], pattern=[[0, 1]], base=0, channel_multiplier=1,
                               allow_small_or_imprecise_dtypes=True))
            own.done(pool.iota(tokid[:], pattern=[[P, TPB]], base=0, channel_multiplier=1,
                               allow_small_or_imprecise_dtypes=True))
            pool.iota(carry[:, TPB, :], pattern=[[N, E]], base=0, channel_multiplier=0,
                      allow_small_or_imprecise_dtypes=True).then_inc(consts_made, 1)
            pool.wait_ge(slots_cleared, 32)

            def scatter(tiles, b):
                plain_wait(pool, rows_ready, b + 1)
                for jt in tiles:
                    for k in range(K):
                        pool.indirect_dma_start(
                            out=slot_dram, out_offset=bass.IndirectOffsetOnAxis(ap=row_i[:, jt, k:k + 1], axis=0),
                            in_=rec[:, jt, k, :], in_offset=None).then_inc(slots_written, 16)

            own.done(pool.memset(half_power[:], -0.5))
            own.done(pool.memset(gx[:, 4:5], 1.0))
            pool.wait_ge(tanh_made, 1)

            def step(beta, j):
                t = tile_at(beta, j, 3)
                if t is not None:
                    pool.wait_ge(var2_ready, t + 1)
                    own.done(pool.tensor_tensor(st2[:, 10:12], st2[:, 8:10], half_power[:], ALU.pow))
                    own.done(pool.tensor_tensor(st2[:, 16:18], st2[:, 10:12], gx[:, 3:5], ALU.mult))
                    pool.tensor_scalar(st2[:, 18:20], st2[:, 16:18], st2[:, 6:7], -1.0, ALU.mult, ALU.mult).then_inc(
                        ln2_ready, 1)
                t = tile_at(beta, j, 2)
                if t is not None:
                    pool.wait_ge(rinv_made, t + 1)
                    pool.tensor_tensor(prob[:].rearrange("p (h s) -> p h s", s=S),
                                       prob[:].rearrange("p (h s) -> p h s", s=S),
                                       mx[:, 2, :].unsqueeze(2).to_broadcast([P, H, S]), ALU.mult).then_inc(probs_ready, 1)
                t = tile_at(beta, j, 3)
                if t is not None:
                    pool.wait_ge(hs_ready, t + 1)
                    wait(pool, base_stored[(j - 3) % 2], beta * 32 + 16 * ((j - 3) // 2))
                    pool.tensor_tensor(base_sb[:, (j - 3) % 2], x2[:], hs[:], ALU.add).then_inc(base1_ready, 1)
                t = tile_at(beta, j, 0)
                if t is not None:
                    pool.wait_ge(var1_ready, t + 1)
                    own.done(pool.tensor_tensor(st1[:, 12:13], st1[:, 8:9], half_power[:, 0:1], ALU.pow))
                    pool.tensor_scalar(st1[:, 13:14], st1[:, 12:13], st1[:, 6:7], -1.0, ALU.mult, ALU.mult).then_inc(
                        ln1_ready, 1)
                if j == 3 and not (isinstance(beta, int) and beta == 0):
                    scatter(range(TPB), beta - 1)

            token_steps(pool, step, [own])

            pool.wait_ge(tix_ready, 1)
            pool.wait_ge(slots_written, 16 * K * TILES)
            slot_blocks = slot_dram.rearrange("(n s) w -> n (s w)", s=P)
            for hf in range(2):
                pool.indirect_dma_start(out=blocks[:, hf], out_offset=None, in_=slot_blocks,
                                        in_offset=bass.IndirectOffsetOnAxis(ap=tix[:, hf, 0:1], axis=0)).then_inc(
                    blocks_loaded, 16)
                pool.indirect_dma_start(out=id1023[:, hf], out_offset=None, in_=slot_dram,
                                        in_offset=bass.IndirectOffsetOnAxis(ap=tix[:, hf, 1:2], axis=0)).then_inc(
                    blocks_loaded, 16)
            pool.wait_ge(tables_ready, 2)
            pool.wait_ge(h_stored, 16 * TILES)
            for q in range(2):
                pool.wait_ge(base_stored[q], 16 * TILES // 2)
            pool.wait_ge(pads_stored, 16)

            def gather(n, q):
                wait(pool, et_made, n - 3)
                own.done(pool.tensor_copy(src4[:, q:q + 1], src_i[:, bass.ds(n, 1)]))
                pool.indirect_dma_start(out=hg[:, q], out_offset=None, in_=h_dram,
                                        in_offset=bass.IndirectOffsetOnAxis(ap=src4[:, q:q + 1], axis=0)).then_inc(
                    hg_loaded[q], 16)

            def add_out(n, q):
                wait(pool, y_added, 16 * n)
                pool.wait_ge(ey_ready, n + 1)
                own.done(pool.tensor_copy(dst1[:], dst_i[:, bass.ds(n, 1)]))
                pool.indirect_dma_start(out=out, out_offset=bass.IndirectOffsetOnAxis(ap=dst1[:], axis=0),
                                        in_=ey[:, q], in_offset=None, compute_op=ALU.add).then_inc(y_added, 16)

            for n in range(4):
                gather(n, n)
            own.restart()
            with pool.Fori(0, MT // 4 - 1) as i:
                for q in range(4):
                    add_out(4 * i + q, q)
                    gather(4 * i + (q + 4), q)
                own.restart()
            for n in range(MT - 4, MT):
                add_out(n, n % 4)
            pool.wait_ge(y_added, 16 * MT)

        @block.scalar
        def _(act):
            copy = ACT.Copy
            act.wait_ge(small_loaded, 16 * 9)
            act.activation(gx[:, 2:4], gx[:, 0:2], ACT.Tanh).then_inc(tanh_made, 1)
            for c in range(2):
                act.wait_ge(ctx_turned, c + 1)
                act.activation(ctxt[:, c], bank[c][:], copy).then_inc(ctx_copied, 1)

            def group(g, q):
                act.wait_ge(kv_made, 2 * g + 1)
                act.activation(kt[:, bass.ds(g, 1)].rearrange("p o n -> p (o n)"), bank[0][:], copy, scale=SCALE).then_inc(kv_copied, 1)
                act.wait_ge(kv_made, 2 * g + 2)
                wait(act, vw_made, B * g)
                act.activation(vt[:, 0], bank[1][:], copy).then_inc(kv_copied, 1)
                act.activation(vt[:, 1].rearrange("k (p q s) -> k p q s", q=2, s=S),
                               ap(bank[1], S, [[512, P], [2 * S, B // 2], [-S, 2], [1, S]]), copy).then_inc(kv_copied, 1)
                if not (isinstance(g, int) and g < 2):
                    act.wait_ge(vw_stored[q], 64 * (g - q))
                for n in range(B):
                    act.wait_ge(vw_made, B * g + (n + 1))
                    act.activation(vw_st[:, q, 0, n % 2, n // 2], bank[2 + n % 4][:], copy,
                                   scale=mask_ft[:, n % 2, n // 2:n // 2 + 1]).then_inc(vw_hi, 1)

            act.wait_ge(masks_made, 2)
            for g in range(2):
                group(g, g)
            with act.Fori(1, G // 2) as i:
                for q in range(2):
                    group(2 * i + q, q)

            for q in range(2):
                act.wait_ge(vw_stored[q], 16 * 8 * G // 2)

            act.wait_ge(shared_split, 2)

            def m_block(c):
                for h4 in range(H // 4):
                    act.wait_ge(wq_turned, (H // 4) * c + (h4 + 1))
                    wait(act, m_made, H * (c - 1) + 4 * h4 + 4)
                    act.activation(wqt[:, h4 * 512:(h4 + 1) * 512], bank[h4 % 2][:], copy).then_inc(wq_copied, 1)
                    for h in range(4 * h4, 4 * h4 + 4):
                        if h == 0:
                            wait(act, m_stored, 32 * c)
                        act.wait_ge(m_made, H * c + (h + 1))
                        act.activation(m_place(0, h), bank[2 + h % 4][:].rearrange("p (a q s) -> p a q s", q=2, s=S),
                                       copy).then_inc(m_hi, 1)

            for c in range(DC):
                m_block(c)

            def step(beta, j):
                t = tile_at(beta, j, 4)
                if t is not None:
                    act.wait_ge(at_made, t + 1)
                    act.activation(sactt[:, 0], ps_t[0][:, 0:I], copy).then_inc(at_hi, 1)
                t = tile_at(beta, j, 3)
                if t is not None:
                    act.wait_ge(ln2_ready, t + 1)
                    wait(act, base1_ready, t)
                    act.activation(hs[:], x2[:], ACT.Identity, bias=st2[:, 18:19], scale=st2[:, 16:17]).then_inc(hs_ready, 1)
                    wait(act, h_stored, 16 * t)
                    wait(act, ht_made, t)
                    act.activation(h_sb[:], x2[:], ACT.Identity, bias=st2[:, 19:20], scale=st2[:, 17:18]).then_inc(
                        hn_ready, 1)
                if j == 3 and not (isinstance(beta, int) and beta == 0):
                    act.wait_ge(rw_shifted, beta)
                    act.activation(posn[:], posn[:], ACT.Exp)
                    act.activation(rw[:, 0], rw[:, 0], ACT.Exp).then_inc(rw_exp, 1)
                t = tile_at(beta, j, 0)
                if t is not None:
                    act.wait_ge(ln1_ready, t + 1)
                    wait(act, xt_made, t)
                    act.activation(xn[:], x_sb[:, j], ACT.Identity, bias=st1[:, 13:14], scale=st1[:, 12:13]).then_inc(
                        xn_ready, 1)
                t = tile_at(beta, j, 3)
                if t is not None:
                    act.wait_ge(ht_made, t + 1)
                    act.activation(ht[:, 0], ps_t[2][:], copy).then_inc(ht_hi, 1)
                t = tile_at(beta, j, 2)
                if t is not None:
                    for half in range(2):
                        act.wait_ge(pt_made, 2 * t + (half + 1))
                        act.activation(pt[:, 0, half * 512:half * 512 + 512], ps_t[half][:], copy).then_inc(pt_hi, 1)
                t = tile_at(beta, j, 0)
                if t is not None:
                    act.wait_ge(xt_made, t + 1)
                    act.activation(xnt[:, 0], ps_t[2][:], copy).then_inc(xt_hi, 1)
                t = tile_at(beta, j, 3)
                if t is not None:
                    act.wait_ge(gu_made, t + 1)
                    wait(act, act_ready, t)
                    act.activation(sth[:], ps_g[:, 0:I], ACT.Tanh, scale=0.5).then_inc(tanh_ready, 1)
                t = tile_at(beta, j, 1)
                if t is not None:
                    act.wait_ge(shifted, t + 1)
                    act.activation(prob[:], prob[:], ACT.Exp).then_inc(exp_made, 1)

            token_steps(act, step)

            def expert_step(v, j):
                if valid(v - 2):
                    act.wait_ge(eat_made, v - 2 + 1)
                    act.activation(eactt[:, j % 2], bank[3][:, 0:I], copy).then_inc(eat_copied, 1)
                if valid(v):
                    act.wait_ge(et_made, v + 1)
                    act.activation(hgt[:, j % 2], bank[2][:], copy).then_inc(et_copied, 1)
                if valid(v - 1):
                    act.wait_ge(egu_made, v - 1 + 1)
                    wait(act, eact_made, v - 2)
                    act.activation(eth[:, (j - 1) % 2], bank[6 + (j - 1) % 2][:, 0:I], ACT.Tanh, scale=0.5).then_inc(
                        eth_made, 1)

            expert_steps(act, expert_step)

        @block.tensor
        def _(pe):
            SPLIT = ((0, 0), (1, 0), (0, 1))
            pe.wait_ge(ident_made, 1)
            pe.wait_ge(small_loaded, 16 * 9)
            for c in range(2):
                for q in range(4):
                    mm = pe.transpose(bank[c][:, q * P:q * P + P], ctx_sb[:, q, c * P:c * P + P], ident[:])
                mm.then_inc(ctx_turned, 1)
            pe.wait_ge(ctx_copied, 2)

            def group(g, q, nth):
                pe.wait_ge(gw_loaded[q], 48 * nth)
                wait(pe, kv_copied, 3 * g)
                for o, w in enumerate((wkg, wvg)):
                    for c in range(2):
                        mm = pe.matmul(bank[o][:], w[:, q, c], ctxt[:, c], start=c == 0, stop=c == 1)
                    mm.then_inc(kv_made, 1)
                pe.wait_ge(kv_copied, 3 * g + 3)
                for n in range(B):
                    wait(pe, vw_split, B * g + (n - 3))
                    mm = pe.matmul(bank[2 + n % 4][:], vt[:, n % 2, (n // 2) * P:(n // 2) * P + P],
                                   wog[:, q, n % 2], start=True, stop=True)
                    mm.then_inc(vw_made, 1)

            for g in range(2):
                group(g, g, 1)
            with pe.Fori(1, G // 2) as i:
                for q in range(2):
                    group(2 * i + q, q, i + 1)

            def turn(c, h4):
                pe.wait_ge(wq_loaded[c % 2], 16 * (c // 2 + 1))
                for h in range(4 * h4, 4 * h4 + 4):
                    mm = pe.transpose(bank[h4 % 2][:, (h % 4) * P:(h % 4) * P + P], wqc[:, c % 2, h * P:h * P + P], ident[:])
                mm.then_inc(wq_turned, 1)

            for c in range(DC):
                for h4 in range(H // 4):
                    if h4 == 0:
                        turn(c, 0)
                    if h4 + 1 < H // 4:
                        turn(c, h4 + 1)
                    pe.wait_ge(wq_copied, 4 * c + h4 + 1)
                    for h in range(4 * h4, 4 * h4 + 4):
                        n = H * c + h
                        wait(pe, m_split, n - 3)
                        if n < 4:
                            pe.wait_ge(vw_split, B * G)
                        pe.matmul(bank[2 + h % 4][:], wqt[:, h * P:h * P + P], kt[:, h // 2], start=True, stop=True
                                  ).then_inc(m_made, 1)
            pe.wait_ge(shared_loaded, 64)
            for c in range(DC):
                mm = pe.transpose(bank[7][:, c * E:c * E + E], x_sb[0:E, 2, c * P:c * P + P], ident[0:E, 0:E])
            mm.then_inc(gate_turned, 1)
            pe.wait_ge(gate_split, 1)
            pe.wait_ge(m_split, H * DC)
            pe.wait_ge(consts_made, 2)

            def scores(t, half, q):
                first = True
                for c in range(DC):
                    for a, m in SPLIT:
                        pe.matmul(ps_s[half][:], xnt[:, a, c * P:c * P + P],
                                  m_sb[:, bass.ds(q, 1), m, c, half * 512:half * 512 + 512].rearrange("p o n -> p (o n)"),
                                  start=first, stop=False)
                        first = False

            def step(beta, j):
                t = tile_at(beta, j, 1)
                b = batch_of(beta, j, 1)
                if t is not None:
                    q = b % 2
                    if j == 1:
                        pe.wait_ge(mw_loaded, b * 32 + 32)
                    pe.wait_ge(xt_split, t + 1)
                    wait(pe, shifted, t)
                    scores(t, 0, q)
                    pe.matmul(ps_s[0][:], row0[:], bias[:, bass.ds(b, 1)].to_broadcast([P, 8, S]), start=False, stop=True)
                td = tile_at(beta, j, 4)
                if td is not None:
                    pe.wait_ge(at_split, td + 1)
                    pe.wait_ge(x2_ready, min(td + 2, TILES) if isinstance(td, int) else td + 2)
                    first = True
                    for c in range(IC):
                        for a, m in SPLIT:
                            mm = pe.matmul(ps_od[:], sactt[:, a, c * P:c * P + P], swd[:, m, c], start=first,
                                           stop=(c == IC - 1 and (a, m) == SPLIT[-1]))
                            first = False
                    mm.then_inc(down_made, 1)
                th = tile_at(beta, j, 3)
                if th is not None:
                    pe.wait_ge(h_ready, th + 1)
                    for c in range(DC):
                        mm = pe.transpose(ps_t[2][:, c * P:c * P + P], h_sb[:, c * P:c * P + P], ident[:])
                    mm.then_inc(ht_made, 1)
                if t is not None:
                    scores(t, 1, q)
                    pe.matmul(ps_s[1][:], row0[:], bias[:, bass.ds(b, 1)].to_broadcast([P, 8, S]), start=False, stop=True
                              ).then_inc(scores_made, 1)
                if j == 3 and not (isinstance(beta, int) and beta == 0):
                    pe.wait_ge(chosen_ready, beta)
                    pe.matmul(ps_l[:, P:2 * P], tri[:], chosen[:].rearrange("p t e -> p (t e)"), start=True, stop=True)
                    pe.matmul(ps_l[:, 2 * P:3 * P], ones[:], chosen[:].rearrange("p t e -> p (t e)"), start=True, stop=True
                              ).then_inc(ranks_made, 1)
                tp = tile_at(beta, j, 2)
                if tp is not None:
                    pe.wait_ge(probs_ready, tp + 1)
                    for half in range(2):
                        for c in range(4):
                            n = 4 * half + c
                            mm = pe.transpose(ps_t[half][:, c * P:c * P + P], prob[:, n * P:n * P + P], ident[:])
                        mm.then_inc(pt_made, 1)
                if th is not None:
                    pe.wait_ge(ht_split, th + 1)
                    wait(pe, logits_kept, th)
                    if j == 3:
                        wait(pe, ranks_kept, beta)
                    first = True
                    for c in range(DC):
                        for a, m in SPLIT:
                            mm = pe.matmul(ps_l[:, 0:E], ht[:, a, c * P:c * P + P], gtw[:, m, c], start=first,
                                           stop=(c == DC - 1 and (a, m) == SPLIT[-1]))
                            first = False
                    mm.then_inc(logits_made, 1)
                    wait(pe, act_ready, th)
                    first = True
                    for c in range(DC):
                        for a, m in SPLIT:
                            mm = pe.matmul(ps_g[:], ht[:, a, c * P:c * P + P], swg[:, m, c], start=first,
                                           stop=(c == DC - 1 and (a, m) == SPLIT[-1]))
                            first = False
                    mm.then_inc(gu_made, 1)
                tx = tile_at(beta, j, 0)
                if tx is not None:
                    pe.wait_ge(xn_ready, tx + 1)
                    for c in range(DC):
                        mm = pe.transpose(ps_t[2][:, c * P:c * P + P], xn[:, c * P:c * P + P], ident[:])
                    mm.then_inc(xt_made, 1)
                if tp is not None:
                    bp = batch_of(beta, j, 2)
                    wait(pe, base_ready, tp - 1)
                    first = True
                    for half in range(2):
                        pe.wait_ge(pt_split, 2 * tp + (half + 1))
                        for c in range(4 * half, 4 * half + 4):
                            for a, m in SPLIT:
                                mm = pe.matmul(ps_od[:], pt[:, a, c * P:c * P + P],
                                               vw_sb[:, bass.ds(bp % 2, 1), m, c].rearrange("p o n -> p (o n)"),
                                               start=first, stop=(c == HC - 1 and (a, m) == SPLIT[-1]))
                                first = False
                    mm.then_inc(attn_made, 1)
                if th is not None:
                    pe.wait_ge(act_ready, th + 1)
                    for c in range(IC):
                        mm = pe.transpose(ps_t[0][:, c * P:c * P + P], sact[:, c * P:c * P + P], ident[:])
                    mm.then_inc(at_made, 1)

            token_steps(pe, step)

            for hf in range(2):
                pe.wait_ge(rec4_ready, hf + 1)
                for r in range(4):
                    mm = pe.transpose(bank[2 + hf][:, r * P:r * P + P], rec4[:, hf, r], ident[:])
                mm.then_inc(rec4_turned, 1)
            pe.wait_ge(tables_ready, 2)
            pe.sem_inc(ed_made, 1)

            def expert_step(v, j):
                if valid(v - 1):
                    n = v - 1
                    e = pe.value_load(exp_i[0:1, bass.ds(n, 1)], min_val=0, max_val=E - 1)
                    pe.wait_ge(ew_loaded, e * 32 + 32)
                    pe.wait_ge(et_copied, n + 1)
                    wait(pe, eact_made, n - 1)
                    q = e % 2
                    for c in range(DC):
                        mm = pe.matmul(bank[6 + (j - 1) % 2][:], hgt[:, (j - 1) % 2, c * P:c * P + P],
                                       ew13[:, bass.ds(q, 1), c].rearrange("p o n -> p (o n)"),
                                       start=c == 0, stop=c == DC - 1)
                    mm.then_inc(egu_made, 1)
                if valid(v - 2):
                    pe.wait_ge(eact_made, v - 2 + 1)
                    for c in range(IC):
                        mm = pe.transpose(bank[3][:, c * P:c * P + P], eact[:, j % 2, c * P:c * P + P], ident[:])
                    mm.then_inc(eat_made, 1)
                if valid(v):
                    pe.wait_ge(hg_loaded[j], 4 * v + (16 - 4 * j))
                    for c in range(DC):
                        mm = pe.transpose(bank[2][:, c * P:c * P + P], hg[:, j, c * P:c * P + P], ident[:])
                    mm.then_inc(et_made, 1)
                if valid(v - 2):
                    n = v - 2
                    pe.wait_ge(eat_copied, n + 1)
                    wait(pe, ey_ready, n - 1)
                    e = pe.value_load(exp_i[0:1, bass.ds(n, 1)], min_val=0, max_val=E - 1)
                    q = e % 2
                    for c in range(IC):
                        mm = pe.matmul(bank[j % 2][:], eactt[:, j % 2, c * P:c * P + P],
                                       ew2[:, bass.ds(q, 1), c].rearrange("p o n -> p (o n)"),
                                       start=c == 0, stop=c == IC - 1)
                    mm.then_inc(ed_made, 1)

            expert_steps(pe, expert_step)

        @block.vector
        def _(dve):
            own = Count(dve, dve_step)
            tt, ts, stt = dve.tensor_tensor, dve.tensor_scalar, dve.scalar_tensor_tensor
            f = lambda a: a.bitcast(F32)
            dve.wait_ge(small_loaded, 16 * 9)
            dve.tensor_copy(mask_ft[:], mask8c[:]).then_inc(masks_made, 1)
            ts(bias[:].rearrange("p b s -> p (b s)"), mask8[:], -1.0, SQUASH, ALU.add, ALU.mult).then_inc(masks_made, 1)
            dve.wait_ge(shared_loaded, 64)
            own.done(dve.tensor_copy(swg[:, 0], wst[:]))
            tt(swg[:, 1], wst[:], f(swg[:, 0]), ALU.subtract).then_inc(shared_split, 1)
            own.done(dve.tensor_copy(swd[:, 0], x_sb[:, 0:2, :]))
            tt(swd[:, 1], x_sb[:, 0:2, :], f(swd[:, 0]), ALU.subtract).then_inc(shared_split, 1)
            dve.wait_ge(shared_split, 2)

            def group(g, q):
                if not (isinstance(g, int) and g < 2):
                    dve.wait_ge(vw_stored[q], 64 * (g - q))
                for n in range(B):
                    dve.wait_ge(vw_hi, B * g + (n + 1))
                    stt(out=vw_st[:, q, 1, n % 2, n // 2], in0=bank[2 + n % 4][:],
                        scalar=mask_ft[:, n % 2, n // 2:n // 2 + 1],
                        in1=f(vw_st[:, q, 0, n % 2, n // 2]), op0=ALU.mult, op1=ALU.subtract).then_inc(vw_split, 1)

            for g in range(2):
                group(g, g)
            with dve.Fori(1, G // 2) as i:
                for q in range(2):
                    group(2 * i + q, q)
            for n in range(H * DC):
                dve.wait_ge(m_hi, n + 1)
                h = n % H
                tt(m_place(1, h), bank[2 + h % 4][:].rearrange("p (a q s) -> p a q s", q=2, s=S), f(m_place(0, h)),
                   ALU.subtract).then_inc(m_split, 1)
            dve.wait_ge(gate_turned, 1)
            own.done(dve.tensor_copy(gtw[:, 0], bank[7][:, 0:DC * E].rearrange("p (c e) -> p c e", e=E)))
            tt(gtw[:, 1], bank[7][:, 0:DC * E].rearrange("p (c e) -> p c e", e=E), f(gtw[:, 0]), ALU.subtract).then_inc(
                gate_split, 1)
            dve.wait_ge(tanh_made, 1)
            dve.wait_ge(consts_made, 2)
            dve.wait_ge(slots_cleared, 32)
            dve.wait_ge(pads_stored, 16)

            def step(beta, j):
                prologue = isinstance(beta, int) and beta == 0
                t = tile_at(beta, j, 4)
                if t is not None:
                    dve.wait_ge(at_hi, t + 1)
                    tt(sactt[:, 1], ps_t[0][:, 0:I], f(sactt[:, 0]), ALU.subtract).then_inc(at_split, 1)
                t = tile_at(beta, j, 3)
                if t is not None:
                    dve.wait_ge(attn_made, t + 1)
                    wait(dve, base1_ready, t)
                    wait(dve, hn_ready, t)
                    stt(out=x2[:], in0=ps_od[:], scalar=gx[:, 2:3], in1=x_sb[:, (j - 3) % 4], op0=ALU.mult,
                        op1=ALU.add).then_inc(x2_ready, 1)
                    dve.wait_ge(x2_ready, t + 1)
                    own.done(dve.bn_stats(st2[:, 0:6], x2[:]))
                    own.done(dve.bn_aggr(st2[:, 6:8], st2[:, 0:6]))
                    ts(st2[:, 8:9], st2[:, 7:8], LN_EPS, None, ALU.add)
                    ts(st2[:, 9:10], st2[:, 7:8], 1.0 + RMS_EPS, LN_EPS * RMS_EPS, ALU.mult, ALU.add).then_inc(var2_ready, 1)
                t = tile_at(beta, j, 2)
                if t is not None:
                    dve.wait_ge(exp_made, t + 1)
                    own.done(dve.tensor_reduce(mx[:, 1, :], prob[:].rearrange("p (h s) -> p h s", s=S), AX_X, ALU.add))
                    wait(dve, probs_ready, t)
                    dve.reciprocal(mx[:, 2, :], mx[:, 1, :]).then_inc(rinv_made, 1)
                t = tile_at(beta, j, 3)
                if t is not None:
                    dve.wait_ge(hn_ready, t + 1)
                    tt(h_sb[:], h_sb[:], normw[:], ALU.mult).then_inc(h_ready, 1)
                t = tile_at(beta, j, 4)
                if t is not None:
                    dve.wait_ge(down_made, t + 1)
                    if isinstance(t, int) and t == TILES - 1:
                        dve.wait_ge(base1_ready, TILES)
                    stt(out=base_sb[:, j % 2], in0=ps_od[:], scalar=gx[:, 3:4], in1=base_sb[:, j % 2], op0=ALU.mult,
                        op1=ALU.add).then_inc(base_ready, 1)
                t = tile_at(beta, j, 0)
                if t is not None:
                    dve.wait_ge(x_loaded[j], 16 * beta + 16)
                    wait(dve, xn_ready, t)
                    own.done(dve.bn_stats(st1[:, 0:6], x_sb[:, j]))
                    own.done(dve.bn_aggr(st1[:, 6:8], st1[:, 0:6]))
                    ts(st1[:, 8:9], st1[:, 7:8], LN_EPS, None, ALU.add).then_inc(var1_ready, 1)
                t = tile_at(beta, j, 3)
                if t is not None:
                    dve.wait_ge(ht_hi, t + 1)
                    tt(ht[:, 1], ps_t[2][:], f(ht[:, 0]), ALU.subtract).then_inc(ht_split, 1)
                if j == 3 and not prologue:
                    dve.wait_ge(ranks_made, beta)
                    dve.tensor_copy(ranks[:], ps_l[:, P:3 * P]).then_inc(ranks_kept, 1)
                t = tile_at(beta, j, 2)
                if t is not None:
                    for half in range(2):
                        dve.wait_ge(pt_hi, 2 * t + (half + 1))
                        tt(pt[:, 1, half * 512:half * 512 + 512], ps_t[half][:], f(pt[:, 0, half * 512:half * 512 + 512]),
                           ALU.subtract).then_inc(pt_split, 1)
                if j == 3 and not prologue:
                    routing_rows(beta)
                t = tile_at(beta, j, 3)
                if t is not None:
                    jt = (j - 3) % 4
                    dve.wait_ge(logits_made, t + 1)
                    own.done(dve.tensor_copy(logit[:, 0, jt], ps_l[:, 0:E]))
                    own.done(dve.max(top8[:, jt], logit[:, 0, jt]))
                    dve.max_index(idx8[:, jt], top8[:, jt], logit[:, 0, jt]).then_inc(logits_kept, 1)
                t = tile_at(beta, j, 0)
                if t is not None:
                    dve.wait_ge(xt_hi, t + 1)
                    tt(xnt[:, 1], ps_t[2][:], f(xnt[:, 0]), ALU.subtract).then_inc(xt_split, 1)
                t = tile_at(beta, j, 3)
                if t is not None:
                    dve.wait_ge(tanh_ready, t + 1)
                    wait(dve, at_made, t)
                    own.done(stt(out=sact[:], in0=sth[:], scalar=1.0, in1=ps_g[:, 0:I], op0=ALU.add, op1=ALU.mult))
                    stt(out=sact[:], in0=sact[:], scalar=0.5, in1=ps_g[:, I:2 * I], op0=ALU.mult, op1=ALU.mult).then_inc(
                        act_ready, 1)
                t = tile_at(beta, j, 1)
                if t is not None:
                    dve.wait_ge(scores_made, t + 1)
                    wait(dve, pt_made, 2 * t)
                    for half in range(2):
                        cut = slice(8 * half, 8 * half + 8)
                        own.done(dve.tensor_reduce(mx[:, 0, cut], ps_s[half][:].rearrange("p (h s) -> p h s", s=S), AX_X,
                                                   ALU.max))
                        ins = tt(prob[:, half * 512:half * 512 + 512].rearrange("p (h s) -> p h s", s=S),
                                 ps_s[half][:].rearrange("p (h s) -> p h s", s=S),
                                 mx[:, 0, cut].unsqueeze(2).to_broadcast([P, 8, S]), ALU.subtract)
                    ins.then_inc(shifted, 1)
                if j == 2 and not prologue:
                    routing_choices(beta)

            def routing_choices(beta):
                wait(dve, logits_kept, TPB * beta)
                dve.tensor_copy(idxf[:], idx8[:, :, 0:K])
                tt(posn[:], logit[:, 0], top8[:, :, 0:1].to_broadcast([P, TPB, E]), ALU.subtract)
                tt(rw[:, 0], top8[:, :, 0:K], top8[:, :, 0:1].to_broadcast([P, TPB, K]), ALU.subtract).then_inc(
                    rw_shifted, 1)
                dve.wait_ge(rw_shifted, beta)
                own.done(tt(onehot[:], iota_e[:].unsqueeze(1).unsqueeze(1).to_broadcast([P, TPB, K, E]),
                            idxf[:].unsqueeze(3).to_broadcast([P, TPB, K, E]), ALU.is_equal))
                with nc.allow_low_precision(reason="sums of at most one 1"):
                    dve.tensor_reduce(chosen[:], onehot[:].rearrange("p t k e -> p t e k"), AX_X, ALU.add).then_inc(
                        chosen_ready, 1)

            def routing_rows(beta):
                dve.wait_ge(rw_exp, beta)
                own.done(dve.tensor_reduce(rws[:, 0], posn[:], AX_X, ALU.add))
                own.done(dve.reciprocal(rws[:, 1], rws[:, 0]))
                own.done(tt(rw[:, 1], rw[:, 0], rws[:, 1].unsqueeze(2).to_broadcast([P, TPB, K]), ALU.mult))
                own.done(dve.tensor_reduce(rws[:, 2], rw[:, 1], AX_X, ALU.add))
                own.done(dve.reciprocal(rws[:, 3], rws[:, 2]))
                wait(dve, slots_written, (beta - 1) * (16 * K * TPB))
                tt(rec[:, :, :, 1], rw[:, 1], rws[:, 3].unsqueeze(2).to_broadcast([P, TPB, K]), ALU.mult)
                dve.tensor_copy(rec[:, :, :, 0], tokid[:].unsqueeze(2).to_broadcast([P, TPB, K]))
                dve.wait_ge(ranks_kept, beta)
                own.done(dve.tensor_copy(carry[:, 0], carry[:, TPB]))
                ts(tokid[:], tokid[:], float(T), None, ALU.add)
                for i in range(TPB):
                    own.done(tt(carry[:, i + 1], carry[:, i], ranks[:, P + i * E:P + i * E + E], ALU.add))
                own.done(tt(posn[:], ranks[:, 0:P].rearrange("p (t e) -> p t e", e=E), carry[:, 0:TPB], ALU.add))
                ranked = logit[:, 1]
                for k in range(K):
                    own.done(tt(ranked, onehot[:, :, k], posn[:], ALU.mult))
                    own.done(dve.tensor_reduce(rw[:, 2, :, k], ranked, AX_X, ALU.add))
                dve.tensor_copy(row_i[:], rw[:, 2]).then_inc(rows_ready, 1)

            token_steps(dve, step, [own])

            dve.wait_ge(attn_made, TILES)
            own.done(stt(out=cnt[:, 0], in0=iota_e[:], scalar=-float(N), in1=carry[:, TPB], op0=ALU.mult, op1=ALU.add))
            own.done(ts(cnt_i[:, 0], cnt[:, 0], float(P - 1), None, ALU.add))
            own.done(dve.tensor_single_scalar(cnt_i[:, 1], cnt_i[:, 0], 7, ALU.arith_shift_right))
            own.done(dve.tensor_copy(cnt[:, 1], cnt_i[:, 1]))
            own.done(dve.memset(cnt[:, 2], 1.0))
            own.done(dve.tensor_tensor_scan(cnt[:, 3], cnt[:, 2], cnt[:, 1], 0.0, ALU.mult, ALU.add))
            own.done(ts(end_i[:], cnt[:, 3], 1.0, None, ALU.add))
            for hf in range(2):
                me = tsm[:, hf]
                own.done(ts(me[:, 0:1], iota_p[:], float(P * hf), None, ALU.add))
                own.done(ts(tcmp[:, hf, 0], cnt[:, 3], me[:, 0:1], None, ALU.is_le))
                own.done(dve.tensor_reduce(me[:, 1:2], tcmp[:, hf, 0], AX_X, ALU.add))
                own.done(tt(tcmp[:, hf, 1], tcmp[:, hf, 0], cnt[:, 3], ALU.mult))
                own.done(dve.tensor_reduce(me[:, 2:3], tcmp[:, hf, 1], AX_X, ALU.max))
                own.done(tt(me[:, 3:4], me[:, 0:1], me[:, 2:3], ALU.subtract))
                own.done(ts(me[:, 4:5], me[:, 1:2], float(BLK), me[:, 3:4], ALU.mult, ALU.add))
                own.done(ts(me[:, 5:6], me[:, 4:5], float(PADBLK), None, ALU.min))
                own.done(ts(me[:, 6:7], me[:, 1:2], float(N), float(CAP - 1), ALU.mult, ALU.add))
                own.done(ts(me[:, 7:8], me[:, 6:7], float(PADBLK * P + P - 1), None, ALU.min))
                own.done(ts(me[:, 8:9], me[:, 3:4], float(CAP // P), None, ALU.is_ge))
                own.done(ts(me[:, 9:10], me[:, 1:2], float(E - 1), None, ALU.min))
                own.done(dve.tensor_copy(tix[:, hf, 0:1], me[:, 5:6]))
                ins = dve.tensor_copy(tix[:, hf, 1:2], me[:, 7:8])
                if hf == 0:
                    own.done(ins)
            ins.then_inc(tix_ready, 1)
            dve.wait_ge(blocks_loaded, 64)
            for hf in range(2):
                me = tsm[:, hf]
                ids = blocks[:, hf].rearrange("p (s w) -> p s w", w=2)[:, :, 0]
                ws = blocks[:, hf].rearrange("p (s w) -> p s w", w=2)[:, :, 1]
                own.done(dve.tensor_copy(rec4[:, hf, 0], ids))
                own.done(ts(rec4[:, hf, 1], ids, id1023[:, hf, 0:1], me[:, 8:9], ALU.subtract, ALU.mult))
                own.done(tt(rec4[:, hf, 1], ids, rec4[:, hf, 1], ALU.subtract))
                own.done(ts(rec4[:, hf, 1], rec4[:, hf, 1], float(N - 1), None, ALU.min))
                own.done(ts(rec4[:, hf, 2], ws, gx[:, 3:4], 0.5, ALU.mult, ALU.mult))
                dve.tensor_copy(rec4[:, hf, 3], me[:, 9:10].to_broadcast([P, P])).then_inc(rec4_ready, 1)
            for hf in range(2):
                dve.wait_ge(rec4_turned, hf + 1)
                cut = slice(hf * P, hf * P + P)
                dve.tensor_copy(dst_i[:, cut], bank[2 + hf][:, 0:P])
                dve.tensor_copy(src_i[:, cut], bank[2 + hf][:, P:2 * P])
                dve.tensor_copy(wcol[:, cut], bank[2 + hf][:, 2 * P:3 * P])
                dve.tensor_copy(exp_i[:, cut], bank[2 + hf][:, 3 * P:4 * P]).then_inc(tables_ready, 1)

            def expert_step(v, j):
                if valid(v - 1):
                    n = v - 1
                    q = (j - 1) % 2
                    dve.wait_ge(eth_made, n + 1)
                    wait(dve, eat_made, n - 1)
                    stt(out=eact[:, q], in0=eth[:, q], scalar=1.0, in1=bank[6 + q][:, 0:I], op0=ALU.add,
                        op1=ALU.mult).then_inc(eg_made, 1)
                    dve.wait_ge(eg_made, n + 1)
                    stt(out=eact[:, q], in0=eact[:, q], scalar=wcol[:, bass.ds(n, 1)], in1=bank[6 + q][:, I:2 * I],
                        op0=ALU.mult, op1=ALU.mult).then_inc(eact_made, 1)
                if valid(v - 2):
                    n = v - 2
                    dve.wait_ge(ed_made, n + 2)
                    wait(dve, y_added, 16 * (n - 3))
                    dve.tensor_copy(ey[:, (j - 2) % 4], bank[j % 2][:]).then_inc(ey_ready, 1)

            expert_steps(dve, expert_step)




_INS = ["x", "ctx_1024", "mask_BxS2_bf1", "g_xattn", "g_ffn", "L0_xattn_Wq", "L0_xattn_Wk", "L0_xattn_Wv",
        "L0_xattn_Wo", "L0_ffn_norm_w", "L0_ffn_gate_w", "L0_ffn_w13", "L0_ffn_w2", "L0_ffn_shared_gate_w",
        "L0_ffn_shared_up_w", "L0_ffn_shared_down_w"]


def kernel(**inputs):
    import numpy as _np
    import concourse.bacc as _bacc
    from concourse import mybir as _mybir
    from concourse.bass_utils import run_bass_kernel_spmd as _run

    nc = _bacc.Bacc("TRN2", target_bir_lowering=False, num_devices=1)
    arrays, args = {}, []
    for name in _INS:
        a = _np.ascontiguousarray(inputs[name])
        if a.dtype == _np.bool_:
            a = a.view(_np.uint8)
        arrays[f"in_{name}_dram"] = a
        args.append(nc.dram_tensor(f"in_{name}_dram", a.shape, _mybir.dt.from_np(a.dtype), kind="ExternalInput").ap())
    args.append(nc.dram_tensor("out_0_dram", (N + P, D), _mybir.dt.float32, kind="ExternalOutput").ap())
    flamingo(nc, *args)
    r = _run(nc, [arrays], core_ids=[0])
    return r.results[0]["out_0_dram"][:N].reshape(B, T, D)
```

```python
import concourse.bass as bass
from concourse import mybir
from contextlib import ExitStack

F32 = mybir.dt.float32
F32R = mybir.dt.float32r
BF16 = mybir.dt.bfloat16
I32 = mybir.dt.int32
U32 = mybir.dt.uint32
U8 = mybir.dt.uint8
ALU = mybir.AluOpType
ACT = mybir.ActivationFunctionType
AX_X = mybir.AxisListType.X

P = 128
B, T, D = 8, 512, 512
S, DV = 64, 256
H, G, DH = 16, 8, 128
E, K, I = 32, 4, 256
N = B * T
TILES = N // P
TPB = T // P
DC = D // P
IC = I // P
HS = H * S
HC = HS // P
CAP = 2 * N * K // E
BLK = N // P
PADBLK = E * BLK
MT = N * K // P + E
MTP = 2 * P
SCALE = float(DH) ** -0.5
LN_EPS, RMS_EPS = 1e-5, 1e-6
SQUASH = 1e30
ARENA = 128 * 1024


def ap(t, offset, dims):
    return bass.AP(tensor=t[:].tensor, offset=offset, ap=dims)


class Count:

    def __init__(self, eng, sem):
        self.eng, self.sem, self.n = eng, sem, 0

    def done(self, ins):
        self.n += 1
        ins.then_inc(self.sem, 1)
        self.eng.wait_ge(self.sem, self.n)

    def restart(self):
        if self.n:
            self.eng.wait_ge(self.sem, self.n)
            self.eng.sem_inc(self.sem, -self.n)
            self.n = 0


def wait(eng, sem, value):
    if not isinstance(value, int) or value > 0:
        eng.wait_ge(sem, value)


def token_steps(eng, body, counts=()):
    for beta in range(2):
        for j in range(TPB):
            body(beta, j)
    for c in counts:
        c.restart()
    with eng.Fori(2, B) as beta:
        for j in range(TPB):
            body(beta, j)
        for c in counts:
            c.restart()
    for j in range(TPB):
        body(B, j)


def tile_at(beta, j, lag):
    t = TPB * beta + (j - lag)
    if isinstance(t, int) and not 0 <= t < TILES:
        return None
    return t


def batch_of(beta, j, lag):
    return beta + (j - lag) // TPB


def flamingo(nc, x, ctx, mask, g_xattn, g_ffn, wq, wk, wv, wo, norm_w, gate_w, w13, w2, sg, su, sdn, out):
    es = ExitStack()
    nc.disable_value_cache = True
    with es:
        base = (nc.sbuf_base + 31) // 32 * 32
        es.enter_context(nc.sbuf_tensor("arena", [P, ARENA // 4], F32))
        KB = 1024

        def at(name, shape, dt, kb):
            return nc.alloc_sbuf_tensor_at(name, shape, dt, offset=base + int(kb * KB))

        def sb(name, shape, dt=F32):
            return es.enter_context(nc.sbuf_tensor(name, shape, dt))

        def dram(name, shape, dt=F32):
            return nc.dram_tensor(name, shape, dt, kind="Internal").ap()

        def sem(name):
            return es.enter_context(nc.semaphore(name))

        m_dram = dram("m_dram", (B, P, DC, HS))
        vw_dram = dram("vw_dram", (B, P, G, D))
        h_dram = dram("h_dram", (N, D))
        slot_dram = dram("slot_dram", ((PADBLK + 1) * P, 2))

        m_sb = at("m_sb", [P, 2, 2, DC, HS], F32R, 0)
        vw_sb = at("vw_sb", [P, 2, 2, G, D], F32R, 64)
        vw_st = at("vw_st", [P, 2, 2, B // 2, D], F32, 0)
        m_st = [at("m_st0", [P, B * HS], F32, 32), at("m_st1", [P, B * HS], F32, 0)]
        kt = at("kt", [P, G, B * S], F32, 64)
        wqc = at("wqc", [P, 2, H * DH], F32, 80)
        wqt = at("wqt", [P, H * P], F32, 96)
        ctx_sb = at("ctx_sb", [P, 4, DV], F32, 104)
        ctxt = at("ctxt", [P, 2, B * S], F32, 108)
        wkg = at("wkg", [P, 2, 2, DH], F32, 112)
        wvg = at("wvg", [P, 2, 2, DH], F32, 114)
        wog = at("wog", [P, 2, 2, D], F32, 116)
        vt = at("vt", [P, 2, 2, B * S], F32, 32)
        wst = at("wst", [P, DC, 2 * I], F32, 40)
        ew13 = at("ew13", [P, 2, DC, 2 * I], F32, 0)
        ew2 = at("ew2", [P, 2, IC, D], F32, 16)
        hg = at("hg", [P, 4, D], F32, 24)
        hgt = at("hgt", [P, 2, D], F32, 32)
        eth = at("eth", [P, 2, I], F32, 36)
        eact = at("eact", [P, 2, I], F32, 38)
        eactt = at("eactt", [P, 2, I], F32, 40)
        ey = at("ey", [P, 4, D], F32, 42)
        blocks = at("blocks", [P, 2, 2 * P], F32, 50)
        rec4 = at("rec4", [P, 2, 4, P], F32, 54)
        dst_i = at("dst_i", [P, MTP], I32, 58)
        src_i = at("src_i", [P, MTP], I32, 59)
        wcol = at("wcol", [P, MTP], F32, 60)
        exp_i = at("exp_i", [P, MTP], I32, 61)
        tcmp = at("tcmp", [P, 2, 2, E], F32, 62)
        tsm = at("tsm", [P, 2, 16], F32, 63)
        id1023 = at("id1023", [P, 2, 2], F32, 64)
        tix = at("tix", [P, 2, 2], I32, 64.25)
        cnt = at("cnt", [P, 4, E], F32, 65)
        cnt_i = at("cnt_i", [P, 2, E], I32, 66)
        end_i = at("end_i", [P, E], I32, 67)
        src4 = at("src4", [P, 4], I32, 68)
        dst1 = at("dst1", [P, 1], I32, 68.25)

        ident = sb("ident", [P, P])
        row0 = sb("row0", [P, P], BF16)
        tri = sb("tri", [P, P], BF16)
        ones = sb("ones", [P, P], BF16)
        iota_e = sb("iota_e", [P, E])
        iota_p = sb("iota_p", [P, 1])
        gx = sb("gx", [P, 5])
        half_power = sb("half_power", [P, 2])
        mask8 = sb("mask8", [P, B * S], U8)
        mask_ft = sb("mask_ft", [P, 2, B // 2])
        mask8c = sb("mask8c", [P, 2, B // 2], U8)
        bias = sb("bias", [P, B, S], BF16)
        normw = sb("normw", [P, D])
        swg = sb("swg", [P, 2, DC, 2 * I], F32R)
        swd = sb("swd", [P, 2, IC, D], F32R)
        gtw = sb("gtw", [P, 2, DC, E], F32R)
        x_sb = sb("x_sb", [P, 4, D])
        xn = sb("xn", [P, D])
        xnt = sb("xnt", [P, 2, D], F32R)
        prob = sb("prob", [P, HS])
        pt = sb("pt", [P, 2, HS], F32R)
        x2 = sb("x2", [P, D])
        hs = sb("hs", [P, D])
        h_sb = sb("h_sb", [P, D])
        ht = sb("ht", [P, 2, D], F32R)
        sth = sb("sth", [P, I])
        sact = sb("sact", [P, I])
        sactt = sb("sactt", [P, 2, I], F32R)
        base_sb = sb("base_sb", [P, 2, D])
        st1 = sb("st1", [P, 16])
        st2 = sb("st2", [P, 24])
        mx = sb("mx", [P, 3, H])
        logit = sb("logit", [P, TPB, E])
        top8 = sb("top8", [P, TPB, 8])
        idx8 = sb("idx8", [P, TPB, 8], U32)
        idxf = sb("idxf", [P, TPB, K])
        onehot = sb("onehot", [P, TPB, K, E], BF16)
        chosen = sb("chosen", [P, TPB, E], BF16)
        carry = sb("carry", [P, TPB + 1, E])
        posn = sb("posn", [P, TPB, E])
        ranks = sb("ranks", [P, 2 * TPB * E])
        rw = sb("rw", [P, 4, TPB, K])
        rws = sb("rws", [P, 4, TPB])
        rec = sb("rec", [P, TPB, K, 2])
        row_i = sb("row_i", [P, TPB, K], I32)
        tokid = sb("tokid", [P, TPB])
        bank = [es.enter_context(nc.psum_tensor(f"bank{i}", [P, 512], F32)) for i in range(8)]
        ps_s = bank[0:2]
        ps_t = bank[2:5]
        ps_od, ps_g, ps_l = bank[5], bank[6], bank[7]

        consts_made, ident_made = sem("consts_made"), sem("ident_made")
        small_loaded, masks_made, tanh_made = sem("small_loaded"), sem("masks_made"), sem("tanh_made")
        shared_loaded, shared_split = sem("shared_loaded"), sem("shared_split")
        gate_turned, gate_split = sem("gate_turned"), sem("gate_split")
        ctx_turned, ctx_copied = sem("ctx_turned"), sem("ctx_copied")
        gw_loaded = [sem("gw_loaded0"), sem("gw_loaded1")]
        wo_loaded = [sem("wo_loaded0"), sem("wo_loaded1")]
        kv_made, kv_copied = sem("kv_made"), sem("kv_copied")
        vw_made, vw_copied = sem("vw_made"), sem("vw_copied")
        vw_stored = [sem("vw_stored0"), sem("vw_stored1")]
        wq_loaded = [sem("wq_loaded0"), sem("wq_loaded1")]
        wq_turned, wq_copied = sem("wq_turned"), sem("wq_copied")
        m_made, m_copied = sem("m_made"), sem("m_copied")
        m_stored = [sem("m_stored0"), sem("m_stored1")]
        dve_step, pool_step = sem("dve_step"), sem("pool_step")
        slots_cleared = sem("slots_cleared")

        x_loaded = [sem(f"x_loaded{i}") for i in range(4)]
        mw_loaded, mw_hi, mw_split_dve, mw_split_pool = (
            sem("mw_loaded"), sem("mw_hi"), sem("mw_split_dve"), sem("mw_split_pool"))
        xn_ready, xt_made, xt_hi, xt_split = sem("xn_ready"), sem("xt_made"), sem("xt_hi"), sem("xt_split")
        var1_ready, ln1_ready, var2_ready = sem("var1_ready"), sem("ln1_ready"), sem("var2_ready")
        scores_made, shifted, exp_made, rinv_made, probs_ready = (
            sem("scores_made"), sem("shifted"), sem("exp_made"), sem("rinv_made"), sem("probs_ready"))
        pt_made, pt_hi, pt_split = sem("pt_made"), sem("pt_hi"), sem("pt_split")
        attn_made, x2_ready, ln2_ready, hs_ready, hn_ready, h_ready = (
            sem("attn_made"), sem("x2_ready"), sem("ln2_ready"), sem("hs_ready"), sem("hn_ready"), sem("h_ready"))
        base1_ready, h_stored = sem("base1_ready"), sem("h_stored")
        ht_made, ht_hi, ht_split = sem("ht_made"), sem("ht_hi"), sem("ht_split")
        logits_made, logits_kept, gu_made, tanh_ready, act_ready = (
            sem("logits_made"), sem("logits_kept"), sem("gu_made"), sem("tanh_ready"), sem("act_ready"))
        at_made, at_hi, at_split = sem("at_made"), sem("at_hi"), sem("at_split")
        down_made, base_ready = sem("down_made"), sem("base_ready")
        base_stored = [sem("base_stored0"), sem("base_stored1")]
        pads_stored = sem("pads_stored")
        ranks_kept = sem("ranks_kept")
        chosen_ready, ranks_made, rw_shifted, rw_exp, rows_ready, slots_written = (
            sem("chosen_ready"), sem("ranks_made"), sem("rw_shifted"), sem("rw_exp"), sem("rows_ready"),
            sem("slots_written"))
        tix_ready, blocks_loaded, rec4_ready, rec4_turned, tables_ready = (
            sem("tix_ready"), sem("blocks_loaded"), sem("rec4_ready"), sem("rec4_turned"), sem("tables_ready"))

        ew_loaded = sem("ew_loaded")
        eg_made = sem("eg_made")
        hg_loaded = [sem(f"hg_loaded{i}") for i in range(4)]
        et_made, et_copied, egu_made, eth_made, eact_made = (
            sem("et_made"), sem("et_copied"), sem("egu_made"), sem("eth_made"), sem("eact_made"))
        eat_made, eat_copied, ed_made, ey_ready, y_added = (
            sem("eat_made"), sem("eat_copied"), sem("ed_made"), sem("ey_ready"), sem("y_added"))

        def plain_wait(eng, sem, value):
            value = value if isinstance(value, int) else eng.snap(value)
            eng.wait_ge(consts_made, 2)
            eng.wait_ge(sem, value)

        x_rows = x.rearrange("b t d -> (b t) d")
        wq_rows = wq.rearrange("(c p) n -> c p n", p=P)
        def m_place(c, h):
            e = h % 2
            return ap(m_st[c % 2], (h // 2) * 2 * S + e * S,
                      [[B * HS, P], [2 * HS, B // 2], [HS + (S if e == 0 else -S), 2], [1, S]])

        def mw_piece(r, i):
            t = m_sb if i < 4 else vw_sb
            flat = t[:].rearrange("p q l c n -> p q l (c n)")[:, bass.ds(r % 2, 1), :, (i % 4) * HS:(i % 4 + 1) * HS]
            return [flat[:, :, l].rearrange("p o n -> p (o n)") for l in range(2)]

        def f(a):
            return a.bitcast(F32)

        MW_STEPS = {0: range(5), 1: range(5, 8)}
        POOL_PIECES = (3, 5, 7)

        def mw_row(beta, j):
            return None if j > 1 or (isinstance(beta, int) and not 1 <= beta < B) else beta

        def valid(n):
            return not isinstance(n, int) or 0 <= n < MT

        def expert_steps(eng, body):
            for v in range(8):
                body(v, v % 4)
            with eng.Fori(2, MT // 4) as i:
                for j in range(4):
                    body(4 * i + j, j)
            for j in range(2):
                body(MT + j, j)

        block = es.enter_context(nc.Block())

        @block.sync
        def _(sp):
            sp.dma_start(ctx_sb[:], ctx.rearrange("b s d -> (b s) d").rearrange("(q p) d -> p q d", p=P)).then_inc(
                small_loaded, 16)
            sp.dma_start(gx[:, 0:1], g_xattn.rearrange("(a n) -> a n", a=1).to_broadcast([P, 1])).then_inc(small_loaded, 16)
            sp.dma_start(gx[:, 1:2], g_ffn.rearrange("(a n) -> a n", a=1).to_broadcast([P, 1])).then_inc(small_loaded, 16)
            sp.dma_start(normw[:], norm_w.rearrange("(a n) -> a n", a=1).to_broadcast([P, D])).then_inc(small_loaded, 16)
            sp.dma_start(mask8[:], mask.rearrange("b s -> (b s)").rearrange("(a n) -> a n", a=1).to_broadcast([P, B * S])
                         ).then_inc(small_loaded, 16)
            by_s = mask.rearrange("(p q) s -> s q p", q=2)
            for odd in range(2):
                for half in range(2):
                    sp.dma_start(mask8c[half * S:half * S + S, odd, :], by_s[:, half ^ odd, :],
                                 allow_slow_non_contiguous=True).then_inc(small_loaded, 16)

            def load_kv(g, q):
                for dst, src in ((wkg, wk), (wvg, wv)):
                    sp.dma_start(dst[:, q], src.rearrange("(c p) (g n) -> g p c n", p=P, n=DH)[bass.ds(g, 1)].rearrange(
                        "o p c n -> p (o c) n")).then_inc(gw_loaded[q], 16)

            def load_wo(g, q):
                sp.dma_start(wog[:, q], wo.rearrange("(g e p) n -> g p e n", e=2, p=P)[bass.ds(g, 1)].rearrange(
                    "o p e n -> p (o e) n")).then_inc(wo_loaded[q], 16)

            def store_group(g, q):
                sp.wait_ge(vw_copied, B * g + B)
                for odd in range(2):
                    for half in range(2):
                        row = vw_dram.rearrange("(p q) r g n -> q r p g n", q=2)[half ^ odd, half * S:half * S + S]
                        sp.dma_start(row[:, :, bass.ds(g, 1), :].rearrange("r p o n -> r (p o) n"),
                                     vw_st[half * S:half * S + S, q, odd]).then_inc(vw_stored[q], 16)

            for g in range(2):
                load_kv(g, g)
                load_wo(g, g)
            wst_g = sg.rearrange("(c p) n -> p c n", p=P)
            sp.dma_start(wst[:, :, 0:I], wst_g).then_inc(shared_loaded, 16)
            sp.dma_start(wst[:, :, I:2 * I], su.rearrange("(c p) n -> p c n", p=P)).then_inc(shared_loaded, 16)
            sp.dma_start(x_sb[:, 0:2, :], sdn.rearrange("(c p) n -> p c n", p=P)).then_inc(shared_loaded, 16)
            sp.dma_start(x_sb[0:E, 2, :], gate_w).then_inc(shared_loaded, 16)
            sp.wait_ge(consts_made, 1)
            slot_src = prob[:, 0:2 * P]
            sp.dma_start(slot_dram[0:PADBLK * P].rearrange("(p k s) w -> p k (s w)", p=P, s=P),
                         ap(prob, 0, [[HS, P], [0, PADBLK // P], [1, 2 * P]])).then_inc(slots_cleared, 16)
            sp.dma_start(slot_dram[PADBLK * P:].rearrange("(o s) w -> o (s w)", o=1), slot_src[0:1]).then_inc(
                slots_cleared, 16)
            sp.dma_start(out[N:N + P, :], ap(prob, 2 * P, [[HS, P], [1, D]])).then_inc(pads_stored, 16)

            with sp.Fori(0, G // 2 - 1) as i:
                for q in range(2):
                    sp.wait_ge(kv_made, 4 * i + (2 * q + 2))
                    load_kv(2 * i + q + 2, q)
                    store_group(2 * i + q, q)
                    load_wo(2 * i + q + 2, q)
            sp.dma_start(wqc[:, 0], wq_rows[0]).then_inc(wq_loaded[0], 16)
            sp.dma_start(wqc[:, 1], wq_rows[1]).then_inc(wq_loaded[1], 16)
            for g in range(G - 2, G):
                store_group(g, g % 2)
            for c in range(DC):
                sp.wait_ge(m_copied, H * c + H)
                if c + 2 < DC:
                    sp.dma_start(wqc[:, c % 2], wq_rows[c + 2]).then_inc(wq_loaded[c % 2], 16)
                sp.dma_start(m_dram[:, :, c].rearrange("b p n -> p b n"),
                             m_st[c % 2][:].rearrange("p (b n) -> p b n", b=B)).then_inc(m_stored[c % 2], 16)
            for q in range(2):
                sp.wait_ge(vw_stored[q], 16 * 4 * G // 2)
                sp.wait_ge(m_stored[q], 16 * DC // 2)

            def load_mw(b):
                q = b % 2
                sp.dma_start(m_sb[:, bass.ds(q, 1), 1].bitcast(F32).rearrange("p o c n -> p (o c) n"),
                             m_dram[bass.ds(b, 1)].rearrange("o p c n -> p (o c) n")).then_inc(mw_loaded, 16)
                sp.dma_start(vw_sb[:, bass.ds(q, 1), 1].bitcast(F32).rearrange("p o g n -> p (o g) n"),
                             vw_dram[bass.ds(b, 1)].rearrange("o p g n -> p (o g) n")).then_inc(mw_loaded, 16)

            sp.wait_ge(shared_split, 2)
            sp.wait_ge(gate_turned, 1)
            sp.dma_start(x_sb[:, 0], x_rows[0:P]).then_inc(x_loaded[0], 16)
            load_mw(0)
            sp.wait_ge(mw_loaded, 32)
            load_mw(1)

            def step(beta, j):
                t = tile_at(beta, j, -1)
                if t is not None:
                    wait(sp, x2_ready, t - 3)
                    sp.dma_start(x_sb[:, (j + 1) % 4], x_rows[bass.ds(t * P, P)]).then_inc(x_loaded[(j + 1) % 4], 16)
                t = tile_at(beta, j, 3)
                if t is not None:
                    sp.wait_ge(h_ready, t + 1)
                    sp.dma_start(h_dram[bass.ds(t * P, P)], h_sb[:]).then_inc(h_stored, 16)
                t = tile_at(beta, j, 4)
                if t is not None:
                    sp.wait_ge(base_ready, t + 1)
                    sp.dma_start(out[bass.ds(t * P, P)], base_sb[:, j % 2]).then_inc(base_stored[j % 2], 16)

            for j in range(TPB):
                step(0, j)
            with sp.Fori(1, B - 1) as beta:
                for j in range(TPB):
                    step(beta, j)
                    if j == 1:
                        sp.wait_ge(attn_made, beta * TPB)
                        sp.wait_ge(mw_loaded, beta * 32 + 32)
                        load_mw(beta + 1)
            for beta in (B - 1, B):
                for j in range(TPB):
                    step(beta, j)

            sp.wait_ge(attn_made, TILES)

            def load_expert(e, q):
                sp.dma_start(ew13[:, q], w13[bass.ds(e, 1)].rearrange("o (c p) n -> p (o c) n", p=P)).then_inc(ew_loaded, 16)
                sp.dma_start(ew2[:, q], w2[bass.ds(e, 1)].rearrange("o (c p) n -> p (o c) n", p=P)).then_inc(ew_loaded, 16)

            for e in range(2):
                if e:
                    sp.wait_ge(ew_loaded, 32 * e)
                load_expert(e, e)
            sp.wait_ge(tables_ready, 2)
            with sp.Fori(1, E // 2) as i:
                for q in range(2):
                    last = sp.value_load(end_i[0:1, bass.ds(2 * i + (q - 2), 1)], min_val=1, max_val=MT + 1)
                    sp.wait_ge(ew_loaded, 64 * i + 32 * q)
                    sp.wait_ge(ed_made, last)
                    load_expert(2 * i + q, q)

        @block.gpsimd
        def _(pool):
            own = Count(pool, pool_step)
            own.done(pool.memset(ident[:], 0.0))
            own.done(pool.affine_select(out=ident[:], in_=ident[:], compare_op=ALU.not_equal, fill=1.0, base=0,
                                        pattern=[[-1, P]], channel_multiplier=1))
            pool.iota(iota_e[:], pattern=[[1, E]], base=0, channel_multiplier=0,
                      allow_small_or_imprecise_dtypes=True).then_inc(ident_made, 1)
            own.done(pool.memset(prob[:], 0.0))
            pool.iota(ap(prob, 0, [[HS, P], [2, P]]), pattern=[[1, P]], base=N, channel_multiplier=0,
                      allow_small_or_imprecise_dtypes=True).then_inc(consts_made, 1)
            own.done(pool.memset(ones[:], 1.0))
            own.done(pool.affine_select(out=row0[:], in_=ones[:], compare_op=ALU.is_equal, fill=0.0, base=0,
                                        pattern=[[0, P]], channel_multiplier=1))
            own.done(pool.affine_select(out=tri[:], in_=ones[:], compare_op=ALU.is_gt, fill=0.0, base=0,
                                        pattern=[[1, P]], channel_multiplier=-1))
            own.done(pool.iota(iota_p[:], pattern=[[0, 1]], base=0, channel_multiplier=1,
                               allow_small_or_imprecise_dtypes=True))
            own.done(pool.iota(tokid[:], pattern=[[P, TPB]], base=0, channel_multiplier=1,
                               allow_small_or_imprecise_dtypes=True))
            pool.iota(carry[:, TPB, :], pattern=[[N, E]], base=0, channel_multiplier=0,
                      allow_small_or_imprecise_dtypes=True).then_inc(consts_made, 1)
            pool.wait_ge(slots_cleared, 32)

            def scatter(jt, b):
                if jt == 0:
                    plain_wait(pool, rows_ready, b + 1)
                for k in range(K):
                    pool.indirect_dma_start(
                        out=slot_dram, out_offset=bass.IndirectOffsetOnAxis(ap=row_i[:, jt, k:k + 1], axis=0),
                        in_=rec[:, jt, k, :], in_offset=None).then_inc(slots_written, 16)

            own.done(pool.memset(half_power[:], -0.5))
            own.done(pool.memset(gx[:, 4:5], 1.0))
            pool.wait_ge(tanh_made, 1)

            def split_mw(r, pieces):
                for i in pieces:
                    if i in POOL_PIECES:
                        hi, lo = mw_piece(r, i)
                        pool.wait_ge(mw_hi, 8 * r + (i + 1))
                        pool.tensor_tensor(lo, f(lo), f(hi), ALU.subtract).then_inc(mw_split_pool, 1)

            split_mw(0, range(8))

            def step(beta, j):
                prologue = isinstance(beta, int) and beta == 0
                t = tile_at(beta, j, 3)
                if t is not None:
                    pool.wait_ge(var2_ready, t + 1)
                    own.done(pool.tensor_tensor(st2[:, 10:12], st2[:, 8:10], half_power[:], ALU.pow))
                    own.done(pool.tensor_tensor(st2[:, 16:18], st2[:, 10:12], gx[:, 3:5], ALU.mult))
                    pool.tensor_scalar(st2[:, 18:20], st2[:, 16:18], st2[:, 6:7], -1.0, ALU.mult, ALU.mult).then_inc(
                        ln2_ready, 1)
                t = tile_at(beta, j, 2)
                if t is not None:
                    pool.wait_ge(rinv_made, t + 1)
                    pool.tensor_tensor(prob[:].rearrange("p (h s) -> p h s", s=S),
                                       prob[:].rearrange("p (h s) -> p h s", s=S),
                                       mx[:, 2, :].unsqueeze(2).to_broadcast([P, H, S]), ALU.mult).then_inc(probs_ready, 1)
                t = tile_at(beta, j, 0)
                if t is not None:
                    pool.wait_ge(var1_ready, t + 1)
                    own.done(pool.tensor_tensor(st1[:, 12:13], st1[:, 8:9], half_power[:, 0:1], ALU.pow))
                    pool.tensor_scalar(st1[:, 13:14], st1[:, 12:13], st1[:, 6:7], -1.0, ALU.mult, ALU.mult).then_inc(
                        ln1_ready, 1)
                t = tile_at(beta, j, 3)
                if t is not None:
                    pool.wait_ge(hs_ready, t + 1)
                    wait(pool, base_stored[(j - 3) % 2], beta * 32 + 16 * ((j - 3) // 2))
                    pool.tensor_tensor(base_sb[:, (j - 3) % 2], x2[:], hs[:], ALU.add).then_inc(base1_ready, 1)
                if j == 3 and not prologue:
                    scatter(0, beta - 1)
                elif j < 3 and not (isinstance(beta, int) and beta < 2):
                    scatter(j + 1, beta - 2)
                if mw_row(beta, j) is not None:
                    split_mw(mw_row(beta, j), MW_STEPS[j])

            token_steps(pool, step, [own])
            for jt in range(1, TPB):
                scatter(jt, B - 1)

            pool.wait_ge(tix_ready, 1)
            pool.wait_ge(slots_written, 16 * K * TILES)
            slot_blocks = slot_dram.rearrange("(n s) w -> n (s w)", s=P)
            for hf in range(2):
                pool.indirect_dma_start(out=blocks[:, hf], out_offset=None, in_=slot_blocks,
                                        in_offset=bass.IndirectOffsetOnAxis(ap=tix[:, hf, 0:1], axis=0)).then_inc(
                    blocks_loaded, 16)
                pool.indirect_dma_start(out=id1023[:, hf], out_offset=None, in_=slot_dram,
                                        in_offset=bass.IndirectOffsetOnAxis(ap=tix[:, hf, 1:2], axis=0)).then_inc(
                    blocks_loaded, 16)
            pool.wait_ge(tables_ready, 2)
            pool.wait_ge(h_stored, 16 * TILES)
            for q in range(2):
                pool.wait_ge(base_stored[q], 16 * TILES // 2)
            pool.wait_ge(pads_stored, 16)

            def gather(n, q):
                wait(pool, et_made, n - 3)
                own.done(pool.tensor_copy(src4[:, q:q + 1], src_i[:, bass.ds(n, 1)]))
                pool.indirect_dma_start(out=hg[:, q], out_offset=None, in_=h_dram,
                                        in_offset=bass.IndirectOffsetOnAxis(ap=src4[:, q:q + 1], axis=0)).then_inc(
                    hg_loaded[q], 16)

            def add_out(n, q):
                wait(pool, y_added, 16 * n)
                pool.wait_ge(ey_ready, n + 1)
                own.done(pool.tensor_copy(dst1[:], dst_i[:, bass.ds(n, 1)]))
                pool.indirect_dma_start(out=out, out_offset=bass.IndirectOffsetOnAxis(ap=dst1[:], axis=0),
                                        in_=ey[:, q], in_offset=None, compute_op=ALU.add).then_inc(y_added, 16)

            for n in range(4):
                gather(n, n)
            for n in range(4):
                add_out(n, n)
                gather(n + 4, n)
            own.restart()
            with pool.Fori(1, MT // 4 - 1) as i:
                for q in range(4):
                    add_out(4 * i + q, q)
                    gather(4 * i + (q + 4), q)
                own.restart()
            for n in range(MT - 4, MT):
                add_out(n, n % 4)
            pool.wait_ge(y_added, 16 * MT)

        @block.scalar
        def _(act):
            copy = ACT.Copy
            act.wait_ge(small_loaded, 16 * 9)
            act.activation(gx[:, 2:4], gx[:, 0:2], ACT.Tanh).then_inc(tanh_made, 1)
            for c in range(2):
                act.wait_ge(ctx_turned, c + 1)
                act.activation(ctxt[:, c], bank[c][:], copy).then_inc(ctx_copied, 1)

            def group(g, q):
                act.wait_ge(kv_made, 2 * g + 1)
                act.activation(kt[:, bass.ds(g, 1)].rearrange("p o n -> p (o n)"), bank[0][:], copy, scale=SCALE).then_inc(kv_copied, 1)
                act.wait_ge(kv_made, 2 * g + 2)
                if not (isinstance(g, int) and g < 2):
                    act.wait_ge(vw_made, B * (g - 1))
                act.activation(vt[:, q, 0], bank[1][:], copy).then_inc(kv_copied, 1)
                act.activation(vt[:, q, 1].rearrange("k (p q s) -> k p q s", q=2, s=S),
                               ap(bank[1], S, [[512, P], [2 * S, B // 2], [-S, 2], [1, S]]), copy).then_inc(kv_copied, 1)

            for g in range(2):
                group(g, g)
            with act.Fori(1, G // 2) as i:
                for q in range(2):
                    group(2 * i + q, q)

            for c in range(DC):
                for h4 in range(H // 4):
                    act.wait_ge(wq_turned, (H // 4) * c + (h4 + 1))
                    wait(act, m_made, H * (c - 1) + 4 * h4 + 4)
                    act.activation(wqt[:, h4 * 512:(h4 + 1) * 512], bank[h4 % 2][:], copy).then_inc(wq_copied, 1)

            def split_mw(r, pieces):
                for i in pieces:
                    hi, lo = mw_piece(r, i)
                    act.wait_ge(mw_loaded, 32 * r + 32)
                    act.activation(hi, f(lo), copy).then_inc(mw_hi, 1)

            split_mw(0, range(8))

            def step(beta, j):
                prologue = isinstance(beta, int) and beta == 0
                t = tile_at(beta, j, 4)
                if t is not None:
                    act.wait_ge(at_made, t + 1)
                    act.activation(sactt[:, 0], ps_t[0][:, 0:I], copy).then_inc(at_hi, 1)
                t = tile_at(beta, j, 3)
                if t is not None:
                    act.wait_ge(ln2_ready, t + 1)
                    wait(act, h_stored, 16 * t)
                    wait(act, ht_made, t)
                    act.activation(h_sb[:], x2[:], ACT.Identity, bias=st2[:, 19:20], scale=st2[:, 17:18]).then_inc(
                        hn_ready, 1)
                    wait(act, base1_ready, t)
                    act.activation(hs[:], x2[:], ACT.Identity, bias=st2[:, 18:19], scale=st2[:, 16:17]).then_inc(hs_ready, 1)
                if j == 3 and not prologue:
                    act.wait_ge(rw_shifted, beta)
                    act.activation(posn[:], posn[:], ACT.Exp)
                    act.activation(rw[:, 0], rw[:, 0], ACT.Exp).then_inc(rw_exp, 1)
                t = tile_at(beta, j, 3)
                if t is not None:
                    act.wait_ge(ht_made, t + 1)
                    act.activation(ht[:, 0], ps_t[2][:], copy).then_inc(ht_hi, 1)
                t = tile_at(beta, j, 2)
                if t is not None:
                    for half in range(2):
                        act.wait_ge(pt_made, 2 * t + (half + 1))
                        act.activation(pt[:, 0, half * 512:half * 512 + 512], ps_t[half][:], copy).then_inc(pt_hi, 1)
                t = tile_at(beta, j, 0)
                if t is not None:
                    act.wait_ge(ln1_ready, t + 1)
                    wait(act, xt_made, t)
                    act.activation(xn[:], x_sb[:, j], ACT.Identity, bias=st1[:, 13:14], scale=st1[:, 12:13]).then_inc(
                        xn_ready, 1)
                t = tile_at(beta, j, 3)
                if t is not None:
                    act.wait_ge(gu_made, t + 1)
                    wait(act, act_ready, t)
                    act.activation(sth[:], ps_g[:, 0:I], ACT.Tanh, scale=0.5).then_inc(tanh_ready, 1)
                t = tile_at(beta, j, 0)
                if t is not None:
                    act.wait_ge(xt_made, t + 1)
                    act.activation(xnt[:, 0], ps_t[2][:], copy).then_inc(xt_hi, 1)
                t = tile_at(beta, j, 1)
                if t is not None:
                    act.wait_ge(shifted, t + 1)
                    act.activation(prob[:], prob[:], ACT.Exp).then_inc(exp_made, 1)
                if mw_row(beta, j) is not None:
                    split_mw(mw_row(beta, j), MW_STEPS[j])

            token_steps(act, step)

            def expert_step(v, j):
                if valid(v):
                    act.wait_ge(et_made, v + 1)
                    wait(act, egu_made, v - 1)
                    act.activation(hgt[:, j % 2], bank[2][:], copy).then_inc(et_copied, 1)
                if valid(v - 2):
                    act.wait_ge(eat_made, v - 2 + 1)
                    act.activation(eactt[:, j % 2], bank[3][:, 0:I], copy).then_inc(eat_copied, 1)
                if valid(v - 1):
                    act.wait_ge(egu_made, v - 1 + 1)
                    wait(act, eact_made, v - 2)
                    act.activation(eth[:, (j - 1) % 2], bank[6 + (j - 1) % 2][:, 0:I], ACT.Tanh, scale=0.5).then_inc(
                        eth_made, 1)

            expert_steps(act, expert_step)

        @block.tensor
        def _(pe):
            SPLIT = ((0, 0), (1, 0), (0, 1))
            pe.wait_ge(ident_made, 1)
            pe.wait_ge(small_loaded, 16 * 9)
            for c in range(2):
                for q in range(4):
                    mm = pe.transpose(bank[c][:, q * P:q * P + P], ctx_sb[:, q, c * P:c * P + P], ident[:])
                mm.then_inc(ctx_turned, 1)
            pe.wait_ge(ctx_copied, 2)

            def keys_values(g, q, nth):
                pe.wait_ge(gw_loaded[q], 32 * nth)
                wait(pe, kv_copied, 3 * g)
                for o, w in enumerate((wkg, wvg)):
                    for c in range(2):
                        mm = pe.matmul(bank[o][:], w[:, q, c], ctxt[:, c], start=c == 0, stop=c == 1)
                    mm.then_inc(kv_made, 1)

            def value_out(g, q, nth):
                pe.wait_ge(wo_loaded[q], 16 * nth)
                pe.wait_ge(kv_copied, 3 * g + 3)
                for n in range(B):
                    wait(pe, vw_copied, B * g + (n - 3))
                    pe.matmul(bank[2 + n % 4][:], vt[:, q, n % 2, (n // 2) * P:(n // 2) * P + P],
                              wog[:, q, n % 2], start=True, stop=True).then_inc(vw_made, 1)

            keys_values(0, 0, 1)
            keys_values(1, 1, 1)
            value_out(0, 0, 1)
            with pe.Fori(1, G // 2) as i:
                keys_values(2 * i, 0, i + 1)
                value_out(2 * i - 1, 1, i)
                keys_values(2 * i + 1, 1, i + 1)
                value_out(2 * i, 0, i + 1)
            value_out(G - 1, 1, G // 2)

            def turn(c, h4):
                if h4 == 0:
                    pe.wait_ge(wq_loaded[c % 2], 16 * (c // 2 + 1))
                for h in range(4 * h4, 4 * h4 + 4):
                    mm = pe.transpose(bank[h4 % 2][:, (h % 4) * P:(h % 4) * P + P], wqc[:, c % 2, h * P:h * P + P], ident[:])
                mm.then_inc(wq_turned, 1)

            turns = [(c, h4) for c in range(DC) for h4 in range(H // 4)]
            turn(*turns[0])
            for n4, (c, h4) in enumerate(turns):
                if n4 + 1 < len(turns):
                    wait(pe, wq_copied, n4)
                    turn(*turns[n4 + 1])
                pe.wait_ge(wq_copied, n4 + 1)
                for h in range(4 * h4, 4 * h4 + 4):
                    n = H * c + h
                    wait(pe, m_copied, n - 3)
                    if n < 4:
                        pe.wait_ge(vw_copied, B * G)
                    pe.matmul(bank[2 + h % 4][:], wqt[:, h * P:h * P + P], kt[:, h // 2], start=True, stop=True
                              ).then_inc(m_made, 1)
            pe.wait_ge(shared_loaded, 64)
            for c in range(DC):
                mm = pe.transpose(bank[7][:, c * E:c * E + E], x_sb[0:E, 2, c * P:c * P + P], ident[0:E, 0:E])
            mm.then_inc(gate_turned, 1)
            pe.wait_ge(gate_split, 1)
            pe.wait_ge(m_copied, H * DC)
            pe.wait_ge(consts_made, 2)

            def scores(t, half, q):
                first = True
                for c in range(DC):
                    for a, m in SPLIT:
                        pe.matmul(ps_s[half][:], xnt[:, a, c * P:c * P + P],
                                  m_sb[:, bass.ds(q, 1), m, c, half * 512:half * 512 + 512].rearrange("p o n -> p (o n)"),
                                  start=first, stop=False)
                        first = False

            def step(beta, j):
                t = tile_at(beta, j, 1)
                b = batch_of(beta, j, 1)
                if t is not None:
                    q = b % 2
                    if j == 1:
                        pe.wait_ge(mw_split_dve, b * 5 + 3)
                        pe.wait_ge(mw_split_pool, b * 3 + 1)
                    pe.wait_ge(xt_split, t + 1)
                    wait(pe, shifted, t)
                    for half in range(2):
                        scores(t, half, q)
                        mm = pe.matmul(ps_s[half][:], row0[:], bias[:, bass.ds(b, 1)].to_broadcast([P, 8, S]), start=False,
                                       stop=True)
                    mm.then_inc(scores_made, 1)
                th = tile_at(beta, j, 3)
                if th is not None:
                    pe.wait_ge(h_ready, th + 1)
                    for c in range(DC):
                        mm = pe.transpose(ps_t[2][:, c * P:c * P + P], h_sb[:, c * P:c * P + P], ident[:])
                    mm.then_inc(ht_made, 1)
                td = tile_at(beta, j, 4)
                if td is not None:
                    pe.wait_ge(at_split, td + 1)
                tp = tile_at(beta, j, 2)
                if tp is not None:
                    pe.wait_ge(probs_ready, tp + 1)
                    for half in range(2):
                        for c in range(4):
                            n = 4 * half + c
                            mm = pe.transpose(ps_t[half][:, c * P:c * P + P], prob[:, n * P:n * P + P], ident[:])
                        mm.then_inc(pt_made, 1)
                if j == 3 and not (isinstance(beta, int) and beta == 0):
                    pe.wait_ge(chosen_ready, beta)
                    pe.matmul(ps_l[:, P:2 * P], tri[:], chosen[:].rearrange("p t e -> p (t e)"), start=True, stop=True)
                    pe.matmul(ps_l[:, 2 * P:3 * P], ones[:], chosen[:].rearrange("p t e -> p (t e)"), start=True, stop=True
                              ).then_inc(ranks_made, 1)
                if td is not None:
                    pe.wait_ge(x2_ready, min(td + 2, TILES) if isinstance(td, int) else td + 2)
                    first = True
                    for c in range(IC):
                        for a, m in SPLIT:
                            mm = pe.matmul(ps_od[:], sactt[:, a, c * P:c * P + P], swd[:, m, c], start=first,
                                           stop=(c == IC - 1 and (a, m) == SPLIT[-1]))
                            first = False
                    mm.then_inc(down_made, 1)
                if th is not None:
                    pe.wait_ge(ht_split, th + 1)
                    wait(pe, logits_kept, th)
                    if j == 3:
                        wait(pe, ranks_kept, beta)
                    first = True
                    for c in range(DC):
                        for a, m in SPLIT:
                            mm = pe.matmul(ps_l[:, 0:E], ht[:, a, c * P:c * P + P], gtw[:, m, c], start=first,
                                           stop=(c == DC - 1 and (a, m) == SPLIT[-1]))
                            first = False
                    mm.then_inc(logits_made, 1)
                    wait(pe, act_ready, th)
                    first = True
                    for c in range(DC):
                        for a, m in SPLIT:
                            mm = pe.matmul(ps_g[:], ht[:, a, c * P:c * P + P], swg[:, m, c], start=first,
                                           stop=(c == DC - 1 and (a, m) == SPLIT[-1]))
                            first = False
                    mm.then_inc(gu_made, 1)
                tx = tile_at(beta, j, 0)
                if tx is not None:
                    pe.wait_ge(xn_ready, tx + 1)
                    for c in range(DC):
                        mm = pe.transpose(ps_t[2][:, c * P:c * P + P], xn[:, c * P:c * P + P], ident[:])
                    mm.then_inc(xt_made, 1)
                if tp is not None:
                    bp = batch_of(beta, j, 2)
                    if j == 2:
                        pe.wait_ge(mw_split_dve, bp * 5 + 5)
                        pe.wait_ge(mw_split_pool, bp * 3 + 3)
                    wait(pe, base_ready, tp - 1)
                    first = True
                    for half in range(2):
                        pe.wait_ge(pt_split, 2 * tp + (half + 1))
                        for c in range(4 * half, 4 * half + 4):
                            for a, m in SPLIT:
                                mm = pe.matmul(ps_od[:], pt[:, a, c * P:c * P + P],
                                               vw_sb[:, bass.ds(bp % 2, 1), m, c].rearrange("p o n -> p (o n)"),
                                               start=first, stop=(c == HC - 1 and (a, m) == SPLIT[-1]))
                                first = False
                    mm.then_inc(attn_made, 1)
                if th is not None:
                    pe.wait_ge(act_ready, th + 1)
                    for c in range(IC):
                        mm = pe.transpose(ps_t[0][:, c * P:c * P + P], sact[:, c * P:c * P + P], ident[:])
                    mm.then_inc(at_made, 1)

            token_steps(pe, step)

            for hf in range(2):
                pe.wait_ge(rec4_ready, hf + 1)
                for r in range(4):
                    mm = pe.transpose(bank[2 + hf][:, r * P:r * P + P], rec4[:, hf, r], ident[:])
                mm.then_inc(rec4_turned, 1)
            pe.wait_ge(tables_ready, 2)
            pe.sem_inc(ed_made, 1)

            def expert_step(v, j):
                if valid(v):
                    pe.wait_ge(hg_loaded[j], 4 * v + (16 - 4 * j))
                    wait(pe, et_copied, v)
                    for c in range(DC):
                        mm = pe.transpose(bank[2][:, c * P:c * P + P], hg[:, j, c * P:c * P + P], ident[:])
                    mm.then_inc(et_made, 1)
                if valid(v - 2):
                    pe.wait_ge(eact_made, v - 2 + 1)
                    for c in range(IC):
                        mm = pe.transpose(bank[3][:, c * P:c * P + P], eact[:, j % 2, c * P:c * P + P], ident[:])
                    mm.then_inc(eat_made, 1)
                if valid(v - 1):
                    n = v - 1
                    e = pe.value_load(exp_i[0:1, bass.ds(n, 1)], min_val=0, max_val=E - 1)
                    pe.wait_ge(ew_loaded, e * 32 + 32)
                    pe.wait_ge(et_copied, n + 1)
                    wait(pe, eact_made, n - 1)
                    q = e % 2
                    for c in range(DC):
                        mm = pe.matmul(bank[6 + (j - 1) % 2][:], hgt[:, (j - 1) % 2, c * P:c * P + P],
                                       ew13[:, bass.ds(q, 1), c].rearrange("p o n -> p (o n)"),
                                       start=c == 0, stop=c == DC - 1)
                    mm.then_inc(egu_made, 1)
                if valid(v - 2):
                    n = v - 2
                    pe.wait_ge(eat_copied, n + 1)
                    wait(pe, ey_ready, n - 1)
                    e = pe.value_load(exp_i[0:1, bass.ds(n, 1)], min_val=0, max_val=E - 1)
                    q = e % 2
                    for c in range(IC):
                        mm = pe.matmul(bank[j % 2][:], eactt[:, j % 2, c * P:c * P + P],
                                       ew2[:, bass.ds(q, 1), c].rearrange("p o n -> p (o n)"),
                                       start=c == 0, stop=c == IC - 1)
                    mm.then_inc(ed_made, 1)

            expert_steps(pe, expert_step)

        @block.vector
        def _(dve):
            own = Count(dve, dve_step)
            tt, ts, stt = dve.tensor_tensor, dve.tensor_scalar, dve.scalar_tensor_tensor
            dve.wait_ge(small_loaded, 16 * 9)
            dve.tensor_copy(mask_ft[:], mask8c[:]).then_inc(masks_made, 1)
            ts(bias[:].rearrange("p b s -> p (b s)"), mask8[:], -1.0, SQUASH, ALU.add, ALU.mult).then_inc(masks_made, 1)
            dve.wait_ge(shared_loaded, 64)
            own.done(dve.tensor_copy(swg[:, 0], wst[:]))
            tt(swg[:, 1], wst[:], f(swg[:, 0]), ALU.subtract).then_inc(shared_split, 1)
            own.done(dve.tensor_copy(swd[:, 0], x_sb[:, 0:2, :]))
            tt(swd[:, 1], x_sb[:, 0:2, :], f(swd[:, 0]), ALU.subtract).then_inc(shared_split, 1)
            dve.wait_ge(shared_split, 2)

            def group(g, q):
                if not (isinstance(g, int) and g < 2):
                    dve.wait_ge(vw_stored[q], 32 * (g - q))
                for n in range(B):
                    dve.wait_ge(vw_made, B * g + (n + 1))
                    ts(vw_st[:, q, n % 2, n // 2], bank[2 + n % 4][:], mask_ft[:, n % 2, n // 2:n // 2 + 1], None,
                       ALU.mult).then_inc(vw_copied, 1)

            for g in range(2):
                group(g, g)
            with dve.Fori(1, G // 2) as i:
                for q in range(2):
                    group(2 * i + q, q)
            for n in range(H * DC):
                c, h = divmod(n, H)
                dve.wait_ge(m_made, n + 1)
                if n == H:
                    for q in range(2):
                        dve.wait_ge(vw_stored[q], 16 * 4 * G // 2)
                if h == 0:
                    wait(dve, m_stored[c % 2], 16 * (c // 2))
                dve.tensor_copy(m_place(c, h), bank[2 + h % 4][:].rearrange("p (a q s) -> p a q s", q=2, s=S)).then_inc(
                    m_copied, 1)
            dve.wait_ge(gate_turned, 1)
            own.done(dve.tensor_copy(gtw[:, 0], bank[7][:, 0:DC * E].rearrange("p (c e) -> p c e", e=E)))
            tt(gtw[:, 1], bank[7][:, 0:DC * E].rearrange("p (c e) -> p c e", e=E), f(gtw[:, 0]), ALU.subtract).then_inc(
                gate_split, 1)
            dve.wait_ge(tanh_made, 1)
            dve.wait_ge(consts_made, 2)
            dve.wait_ge(slots_cleared, 32)
            dve.wait_ge(pads_stored, 16)

            def split_mw(r, pieces):
                for i in pieces:
                    if i not in POOL_PIECES:
                        hi, lo = mw_piece(r, i)
                        dve.wait_ge(mw_hi, 8 * r + (i + 1))
                        tt(lo, f(lo), f(hi), ALU.subtract).then_inc(mw_split_dve, 1)

            split_mw(0, range(8))

            def step(beta, j):
                prologue = isinstance(beta, int) and beta == 0
                t = tile_at(beta, j, 3)
                if t is not None:
                    dve.wait_ge(attn_made, t + 1)
                    wait(dve, base1_ready, t)
                    wait(dve, hn_ready, t)
                    stt(out=x2[:], in0=ps_od[:], scalar=gx[:, 2:3], in1=x_sb[:, (j - 3) % 4], op0=ALU.mult,
                        op1=ALU.add).then_inc(x2_ready, 1)
                    dve.wait_ge(x2_ready, t + 1)
                    own.done(dve.bn_stats(st2[:, 0:6], x2[:]))
                    own.done(dve.bn_aggr(st2[:, 6:8], st2[:, 0:6]))
                    ts(st2[:, 8:9], st2[:, 7:8], LN_EPS, None, ALU.add)
                    ts(st2[:, 9:10], st2[:, 7:8], 1.0 + RMS_EPS, LN_EPS * RMS_EPS, ALU.mult, ALU.add).then_inc(var2_ready, 1)
                t = tile_at(beta, j, 4)
                if t is not None:
                    dve.wait_ge(at_hi, t + 1)
                    tt(sactt[:, 1], ps_t[0][:, 0:I], f(sactt[:, 0]), ALU.subtract).then_inc(at_split, 1)
                t = tile_at(beta, j, 2)
                if t is not None:
                    dve.wait_ge(exp_made, t + 1)
                    own.done(dve.tensor_reduce(mx[:, 1, :], prob[:].rearrange("p (h s) -> p h s", s=S), AX_X, ALU.add))
                    wait(dve, probs_ready, t)
                    dve.reciprocal(mx[:, 2, :], mx[:, 1, :]).then_inc(rinv_made, 1)
                t = tile_at(beta, j, 3)
                if t is not None:
                    dve.wait_ge(hn_ready, t + 1)
                    tt(h_sb[:], h_sb[:], normw[:], ALU.mult).then_inc(h_ready, 1)
                t = tile_at(beta, j, 0)
                if t is not None:
                    dve.wait_ge(x_loaded[j], 16 * beta + 16)
                    wait(dve, xn_ready, t)
                    own.done(dve.bn_stats(st1[:, 0:6], x_sb[:, j]))
                    own.done(dve.bn_aggr(st1[:, 6:8], st1[:, 0:6]))
                    ts(st1[:, 8:9], st1[:, 7:8], LN_EPS, None, ALU.add).then_inc(var1_ready, 1)
                t = tile_at(beta, j, 3)
                if t is not None:
                    dve.wait_ge(ht_hi, t + 1)
                    tt(ht[:, 1], ps_t[2][:], f(ht[:, 0]), ALU.subtract).then_inc(ht_split, 1)
                if j == 3 and not prologue:
                    dve.wait_ge(ranks_made, beta)
                    dve.tensor_copy(ranks[:], ps_l[:, P:3 * P]).then_inc(ranks_kept, 1)
                t = tile_at(beta, j, 2)
                if t is not None:
                    for half in range(2):
                        dve.wait_ge(pt_hi, 2 * t + (half + 1))
                        tt(pt[:, 1, half * 512:half * 512 + 512], ps_t[half][:], f(pt[:, 0, half * 512:half * 512 + 512]),
                           ALU.subtract).then_inc(pt_split, 1)
                t = tile_at(beta, j, 4)
                if t is not None:
                    dve.wait_ge(down_made, t + 1)
                    if isinstance(t, int) and t == TILES - 1:
                        dve.wait_ge(base1_ready, TILES)
                    stt(out=base_sb[:, j % 2], in0=ps_od[:], scalar=gx[:, 3:4], in1=base_sb[:, j % 2], op0=ALU.mult,
                        op1=ALU.add).then_inc(base_ready, 1)
                t = tile_at(beta, j, 3)
                if t is not None:
                    jt = (j - 3) % 4
                    dve.wait_ge(logits_made, t + 1)
                    own.done(dve.tensor_copy(logit[:, jt], ps_l[:, 0:E]))
                    own.done(dve.max(top8[:, jt], logit[:, jt]))
                    dve.max_index(idx8[:, jt], top8[:, jt], logit[:, jt]).then_inc(logits_kept, 1)
                t = tile_at(beta, j, 1)
                if t is not None:
                    dve.wait_ge(scores_made, t + 1)
                    for half in range(2):
                        own.done(dve.tensor_reduce(mx[:, 0, 8 * half:8 * half + 8],
                                                   ps_s[half][:].rearrange("p (h s) -> p h s", s=S), AX_X, ALU.max))
                    wait(dve, pt_made, 2 * t)
                    for half in range(2):
                        ins = tt(prob[:, half * 512:half * 512 + 512].rearrange("p (h s) -> p h s", s=S),
                                 ps_s[half][:].rearrange("p (h s) -> p h s", s=S),
                                 mx[:, 0, 8 * half:8 * half + 8].unsqueeze(2).to_broadcast([P, 8, S]), ALU.subtract)
                    ins.then_inc(shifted, 1)
                t = tile_at(beta, j, 3)
                if t is not None:
                    dve.wait_ge(tanh_ready, t + 1)
                    wait(dve, at_made, t)
                    own.done(stt(out=sact[:], in0=sth[:], scalar=1.0, in1=ps_g[:, 0:I], op0=ALU.add, op1=ALU.mult))
                    stt(out=sact[:], in0=sact[:], scalar=0.5, in1=ps_g[:, I:2 * I], op0=ALU.mult, op1=ALU.mult).then_inc(
                        act_ready, 1)
                t = tile_at(beta, j, 0)
                if t is not None:
                    dve.wait_ge(xt_hi, t + 1)
                    tt(xnt[:, 1], ps_t[2][:], f(xnt[:, 0]), ALU.subtract).then_inc(xt_split, 1)
                if j == 2 and not prologue:
                    routing_choices(beta)
                if j == 3 and not prologue:
                    routing_rows(beta)
                if mw_row(beta, j) is not None:
                    split_mw(mw_row(beta, j), MW_STEPS[j])

            def routing_choices(beta):
                wait(dve, logits_kept, TPB * beta)
                dve.tensor_copy(idxf[:], idx8[:, :, 0:K])
                tt(posn[:], logit[:], top8[:, :, 0:1].to_broadcast([P, TPB, E]), ALU.subtract)
                tt(rw[:, 0], top8[:, :, 0:K], top8[:, :, 0:1].to_broadcast([P, TPB, K]), ALU.subtract).then_inc(
                    rw_shifted, 1)
                dve.wait_ge(rw_shifted, beta)
                own.done(tt(onehot[:], iota_e[:].unsqueeze(1).unsqueeze(1).to_broadcast([P, TPB, K, E]),
                            idxf[:].unsqueeze(3).to_broadcast([P, TPB, K, E]), ALU.is_equal))
                with nc.allow_low_precision(reason="sums of at most one 1"):
                    dve.tensor_reduce(chosen[:], onehot[:].rearrange("p t k e -> p t e k"), AX_X, ALU.add).then_inc(
                        chosen_ready, 1)

            def routing_rows(beta):
                dve.wait_ge(rw_exp, beta)
                own.done(dve.tensor_reduce(rws[:, 0], posn[:], AX_X, ALU.add))
                own.done(dve.reciprocal(rws[:, 1], rws[:, 0]))
                own.done(tt(rw[:, 1], rw[:, 0], rws[:, 1].unsqueeze(2).to_broadcast([P, TPB, K]), ALU.mult))
                own.done(dve.tensor_reduce(rws[:, 2], rw[:, 1], AX_X, ALU.add))
                own.done(dve.reciprocal(rws[:, 3], rws[:, 2]))
                wait(dve, slots_written, (beta - 1) * (16 * K * TPB))
                tt(rec[:, :, :, 1], rw[:, 1], rws[:, 3].unsqueeze(2).to_broadcast([P, TPB, K]), ALU.mult)
                dve.tensor_copy(rec[:, :, :, 0], tokid[:].unsqueeze(2).to_broadcast([P, TPB, K]))
                dve.wait_ge(ranks_kept, beta)
                own.done(dve.tensor_copy(carry[:, 0], carry[:, TPB]))
                ts(tokid[:], tokid[:], float(T), None, ALU.add)
                for i in range(TPB):
                    own.done(tt(carry[:, i + 1], carry[:, i], ranks[:, P + i * E:P + i * E + E], ALU.add))
                own.done(tt(posn[:], ranks[:, 0:P].rearrange("p (t e) -> p t e", e=E), carry[:, 0:TPB], ALU.add))
                dve.wait_ge(base1_ready, min(TPB * beta + 1, TILES) if isinstance(beta, int) else TPB * beta + 1)
                marks = hs[:].rearrange("p (t k e) -> p t k e", k=K, e=E)
                own.done(tt(marks, onehot[:], posn[:].unsqueeze(2).to_broadcast([P, TPB, K, E]), ALU.mult))
                own.done(dve.tensor_reduce(rw[:, 2], marks, AX_X, ALU.add))
                dve.tensor_copy(row_i[:], rw[:, 2]).then_inc(rows_ready, 1)

            token_steps(dve, step, [own])

            dve.wait_ge(attn_made, TILES)
            own.done(stt(out=cnt[:, 0], in0=iota_e[:], scalar=-float(N), in1=carry[:, TPB], op0=ALU.mult, op1=ALU.add))
            own.done(ts(cnt_i[:, 0], cnt[:, 0], float(P - 1), None, ALU.add))
            own.done(dve.tensor_single_scalar(cnt_i[:, 1], cnt_i[:, 0], 7, ALU.arith_shift_right))
            own.done(dve.tensor_copy(cnt[:, 1], cnt_i[:, 1]))
            own.done(dve.memset(cnt[:, 2], 1.0))
            own.done(dve.tensor_tensor_scan(cnt[:, 3], cnt[:, 2], cnt[:, 1], 0.0, ALU.mult, ALU.add))
            own.done(ts(end_i[:], cnt[:, 3], 1.0, None, ALU.add))
            for hf in range(2):
                me = tsm[:, hf]
                own.done(ts(me[:, 0:1], iota_p[:], float(P * hf), None, ALU.add))
                own.done(ts(tcmp[:, hf, 0], cnt[:, 3], me[:, 0:1], None, ALU.is_le))
                own.done(dve.tensor_reduce(me[:, 1:2], tcmp[:, hf, 0], AX_X, ALU.add))
                own.done(tt(tcmp[:, hf, 1], tcmp[:, hf, 0], cnt[:, 3], ALU.mult))
                own.done(dve.tensor_reduce(me[:, 2:3], tcmp[:, hf, 1], AX_X, ALU.max))
                own.done(tt(me[:, 3:4], me[:, 0:1], me[:, 2:3], ALU.subtract))
                own.done(ts(me[:, 4:5], me[:, 1:2], float(BLK), me[:, 3:4], ALU.mult, ALU.add))
                own.done(ts(me[:, 5:6], me[:, 4:5], float(PADBLK), None, ALU.min))
                own.done(ts(me[:, 6:7], me[:, 1:2], float(N), float(CAP - 1), ALU.mult, ALU.add))
                own.done(ts(me[:, 7:8], me[:, 6:7], float(PADBLK * P + P - 1), None, ALU.min))
                own.done(ts(me[:, 8:9], me[:, 3:4], float(CAP // P), None, ALU.is_ge))
                own.done(ts(me[:, 9:10], me[:, 1:2], float(E - 1), None, ALU.min))
                own.done(dve.tensor_copy(tix[:, hf, 0:1], me[:, 5:6]))
                ins = dve.tensor_copy(tix[:, hf, 1:2], me[:, 7:8])
                if hf == 0:
                    own.done(ins)
            ins.then_inc(tix_ready, 1)
            dve.wait_ge(blocks_loaded, 64)
            for hf in range(2):
                me = tsm[:, hf]
                ids = blocks[:, hf].rearrange("p (s w) -> p s w", w=2)[:, :, 0]
                ws = blocks[:, hf].rearrange("p (s w) -> p s w", w=2)[:, :, 1]
                own.done(dve.tensor_copy(rec4[:, hf, 0], ids))
                own.done(ts(rec4[:, hf, 1], ids, id1023[:, hf, 0:1], me[:, 8:9], ALU.subtract, ALU.mult))
                own.done(tt(rec4[:, hf, 1], ids, rec4[:, hf, 1], ALU.subtract))
                own.done(ts(rec4[:, hf, 1], rec4[:, hf, 1], float(N - 1), None, ALU.min))
                own.done(ts(rec4[:, hf, 2], ws, gx[:, 3:4], 0.5, ALU.mult, ALU.mult))
                dve.tensor_copy(rec4[:, hf, 3], me[:, 9:10].to_broadcast([P, P])).then_inc(rec4_ready, 1)
            for hf in range(2):
                dve.wait_ge(rec4_turned, hf + 1)
                cut = slice(hf * P, hf * P + P)
                dve.tensor_copy(dst_i[:, cut], bank[2 + hf][:, 0:P])
                dve.tensor_copy(src_i[:, cut], bank[2 + hf][:, P:2 * P])
                dve.tensor_copy(wcol[:, cut], bank[2 + hf][:, 2 * P:3 * P])
                dve.tensor_copy(exp_i[:, cut], bank[2 + hf][:, 3 * P:4 * P]).then_inc(tables_ready, 1)

            def expert_step(v, j):
                if valid(v - 1):
                    n = v - 1
                    q = (j - 1) % 2
                    dve.wait_ge(eth_made, n + 1)
                    wait(dve, eat_made, n - 1)
                    stt(out=eact[:, q], in0=eth[:, q], scalar=1.0, in1=bank[6 + q][:, 0:I], op0=ALU.add,
                        op1=ALU.mult).then_inc(eg_made, 1)
                    dve.wait_ge(eg_made, n + 1)
                    stt(out=eact[:, q], in0=eact[:, q], scalar=wcol[:, bass.ds(n, 1)], in1=bank[6 + q][:, I:2 * I],
                        op0=ALU.mult, op1=ALU.mult).then_inc(eact_made, 1)
                if valid(v - 2):
                    n = v - 2
                    dve.wait_ge(ed_made, n + 2)
                    wait(dve, y_added, 16 * (n - 3))
                    dve.tensor_copy(ey[:, (j - 2) % 4], bank[j % 2][:]).then_inc(ey_ready, 1)

            expert_steps(dve, expert_step)




_INS = ["x", "ctx_1024", "mask_BxS2_bf1", "g_xattn", "g_ffn", "L0_xattn_Wq", "L0_xattn_Wk", "L0_xattn_Wv",
        "L0_xattn_Wo", "L0_ffn_norm_w", "L0_ffn_gate_w", "L0_ffn_w13", "L0_ffn_w2", "L0_ffn_shared_gate_w",
        "L0_ffn_shared_up_w", "L0_ffn_shared_down_w"]


def kernel(**inputs):
    import numpy as _np
    import concourse.bacc as _bacc
    from concourse import mybir as _mybir
    from concourse.bass_utils import run_bass_kernel_spmd as _run

    nc = _bacc.Bacc("TRN2", target_bir_lowering=False, num_devices=1)
    arrays, args = {}, []
    for name in _INS:
        a = _np.ascontiguousarray(inputs[name])
        if a.dtype == _np.bool_:
            a = a.view(_np.uint8)
        arrays[f"in_{name}_dram"] = a
        args.append(nc.dram_tensor(f"in_{name}_dram", a.shape, _mybir.dt.from_np(a.dtype), kind="ExternalInput").ap())
    args.append(nc.dram_tensor("out_0_dram", (N + P, D), _mybir.dt.float32, kind="ExternalOutput").ap())
    flamingo(nc, *args)
    r = _run(nc, [arrays], core_ids=[0])
    return r.results[0]["out_0_dram"][:N].reshape(B, T, D)
```
